# Optimizing a Trainium2 kernel written in Bass

```python
import numpy as np
import jax
import jax.numpy as jnp

def _softmax(x, axis=-1):
    return jax.nn.softmax(x, axis=axis)

def _gelu(x):
    return jax.nn.gelu(x, approximate=True)

def _silu(x):
    return jax.nn.silu(x)

def _sigmoid(x):
    return jax.nn.sigmoid(x)

def _layernorm(x, axis=-1, eps=1e-05):
    m = jnp.mean(x, axis=axis, keepdims=True)
    v = jnp.var(x, axis=axis, keepdims=True)
    return (x - m) / jnp.sqrt(v + eps)

def _scatter_add(tgt, idx, src, axis=0):
    return tgt.at[idx].add(src)

def _segment_sum(src, seg, n):
    return jax.ops.segment_sum(src, seg, n)
kernel_name = 'mk_vit_tower_d1_tok_img256_r4_7facf1'

def setup_inputs(seed: int=0):
    np.random.seed(seed)
    _w = jnp.asarray

    def _rec_inputs():
        import jax
        import jax.numpy as jnp
        _rk = jax.random.key(seed)
        x = -0.000596345 + 1.00056 * jax.random.normal(jax.random.fold_in(_rk, 1), (64, 64, 64, 3), jnp.float32)
        return x
    x = _rec_inputs()

    def _L0_tok_setup():
        import jax, jax.numpy as jnp
        import numpy as np
        M1 = 20
        M2 = 20

        def _spectral_conv(x, w):
            B, Cin, H, W = x.shape
            x_ft = jnp.fft.rfft2(x, norm='ortho')
            out = jnp.einsum('bixy,ioxy->boxy', x_ft[:, :, :M1, :M2], w.astype(x_ft.dtype))
            out_ft = jnp.zeros((B, w.shape[1], H, W // 2 + 1), dtype=x_ft.dtype)
            out_ft = out_ft.at[:, :, :M1, :M2].set(out)
            return jnp.fft.irfft2(out_ft, s=(H, W), norm='ortho')

        def _gelu(x):
            return jax.nn.gelu(x, approximate=False)
        key = jax.random.key(seed)
        ks = jax.random.split(key, 16)
        B, H, W, width = (16, 64, 64, 32)
        scale = 1.0 / (width * width)
        d = {}
        d['coords'] = jax.random.normal(ks[0], (B, H, W, 3), dtype=jnp.float32)
        d['fc0_w'] = jax.random.normal(ks[1], (3, width), dtype=jnp.float32) * 0.1
        d['fc0_b'] = jnp.zeros((width,), dtype=jnp.float32)
        for i in range(4):
            d[f'sw{i}'] = scale * jax.random.normal(ks[2 + i], (width, width, M1, M2), dtype=jnp.float32)
            d[f'cw{i}'] = jax.random.normal(ks[6 + i], (width, width), dtype=jnp.float32) * 0.1
            d[f'cb{i}'] = jnp.zeros((width,), dtype=jnp.float32)
        d['fc1_w'] = jax.random.normal(ks[10], (width, 64), dtype=jnp.float32) * 0.1
        d['fc1_b'] = jnp.zeros((64,), dtype=jnp.float32)
        d['fc2_w'] = jax.random.normal(ks[11], (64, 1), dtype=jnp.float32) * 0.1
        d['fc2_b'] = jnp.zeros((1,), dtype=jnp.float32)
        return d
    _L0_tok_all = _L0_tok_setup()
    _L0_tok_in = {k: v for k, v in _L0_tok_all.items() if k in ('fc0_w', 'fc0_b', 'sw0', 'cw0', 'cb0', 'sw1', 'cw1', 'cb1', 'sw2', 'cw2', 'cb2', 'sw3', 'cw3', 'cb3', 'fc1_w', 'fc1_b', 'fc2_w', 'fc2_b')}
    del _L0_tok_all

    def _L0_attn_setup():
        import jax, jax.numpy as jnp
        import numpy as np
        import math
        B, S, D = (4, 1024, 64)
        key = jax.random.key(seed)
        ks = jax.random.split(key, 9)
        s = 1.0 / math.sqrt(D)
        return {'src': jax.random.normal(ks[0], (B, S, D), dtype=jnp.float32), 'Wq': jax.random.normal(ks[1], (D, D), dtype=jnp.float32) * s, 'bq': jax.random.normal(ks[2], (D,), dtype=jnp.float32) * s, 'Wk': jax.random.normal(ks[3], (D, D), dtype=jnp.float32) * s, 'bk': jax.random.normal(ks[4], (D,), dtype=jnp.float32) * s, 'Wv': jax.random.normal(ks[5], (D, D), dtype=jnp.float32) * s, 'bv': jax.random.normal(ks[6], (D,), dtype=jnp.float32) * s, 'Wo': jax.random.normal(ks[7], (D, D), dtype=jnp.float32) * s, 'bo': jax.random.normal(ks[8], (D,), dtype=jnp.float32) * s}
    _L0_attn_all = _L0_attn_setup()
    _L0_attn_in = {k: v for k, v in _L0_attn_all.items() if k in ('Wq', 'bq', 'Wk', 'bk', 'Wv', 'bv', 'Wo', 'bo')}
    del _L0_attn_all

    def _L0_ffn_setup():
        import jax, jax.numpy as jnp
        import numpy as np
        B, S, H, F, E, K = (8, 1024, 64, 128, 16, 2)
        EPS = 1e-05
        key = jax.random.key(seed)
        ks = jax.random.split(key, 9)
        sc = 0.02
        return {'x': jax.random.normal(ks[0], (B, S, H), dtype=jnp.float32), 'gate_w': jax.random.normal(ks[1], (H, E), dtype=jnp.float32) * sc, 'gate_b': jnp.zeros((E,), dtype=jnp.float32), 'w1': jax.random.normal(ks[2], (E, H, F), dtype=jnp.float32) * sc, 'b1': jnp.zeros((E, F), dtype=jnp.float32), 'w2': jax.random.normal(ks[3], (E, F, H), dtype=jnp.float32) * sc, 'b2': jnp.zeros((E, H), dtype=jnp.float32), 'gamma': jnp.ones((H,), dtype=jnp.float32), 'beta': jnp.zeros((H,), dtype=jnp.float32)}
    _L0_ffn_all = _L0_ffn_setup()
    _L0_ffn_in = {k: v for k, v in _L0_ffn_all.items() if k in ('gate_w', 'gate_b', 'w1', 'b1', 'w2', 'b2', 'gamma', 'beta')}
    del _L0_ffn_all
    return {'x': x, 'L0_tok_fc0_w': _L0_tok_in['fc0_w'], 'L0_tok_fc0_b': _L0_tok_in['fc0_b'], 'L0_tok_sw0': _L0_tok_in['sw0'], 'L0_tok_cw0': _L0_tok_in['cw0'], 'L0_tok_cb0': _L0_tok_in['cb0'], 'L0_tok_sw1': _L0_tok_in['sw1'], 'L0_tok_cw1': _L0_tok_in['cw1'], 'L0_tok_cb1': _L0_tok_in['cb1'], 'L0_tok_sw2': _L0_tok_in['sw2'], 'L0_tok_cw2': _L0_tok_in['cw2'], 'L0_tok_cb2': _L0_tok_in['cb2'], 'L0_tok_sw3': _L0_tok_in['sw3'], 'L0_tok_cw3': _L0_tok_in['cw3'], 'L0_tok_cb3': _L0_tok_in['cb3'], 'L0_tok_fc1_w': _L0_tok_in['fc1_w'], 'L0_tok_fc1_b': _L0_tok_in['fc1_b'], 'L0_tok_fc2_w': _L0_tok_in['fc2_w'], 'L0_tok_fc2_b': _L0_tok_in['fc2_b'], 'L0_attn_Wq': _L0_attn_in['Wq'], 'L0_attn_bq': _L0_attn_in['bq'], 'L0_attn_Wk': _L0_attn_in['Wk'], 'L0_attn_bk': _L0_attn_in['bk'], 'L0_attn_Wv': _L0_attn_in['Wv'], 'L0_attn_bv': _L0_attn_in['bv'], 'L0_attn_Wo': _L0_attn_in['Wo'], 'L0_attn_bo': _L0_attn_in['bo'], 'L0_ffn_gate_w': _L0_ffn_in['gate_w'], 'L0_ffn_gate_b': _L0_ffn_in['gate_b'], 'L0_ffn_w1': _L0_ffn_in['w1'], 'L0_ffn_b1': _L0_ffn_in['b1'], 'L0_ffn_w2': _L0_ffn_in['w2'], 'L0_ffn_b2': _L0_ffn_in['b2'], 'L0_ffn_gamma': _L0_ffn_in['gamma'], 'L0_ffn_beta': _L0_ffn_in['beta']}

def reference(x, L0_tok_fc0_w, L0_tok_fc0_b, L0_tok_sw0, L0_tok_cw0, L0_tok_cb0, L0_tok_sw1, L0_tok_cw1, L0_tok_cb1, L0_tok_sw2, L0_tok_cw2, L0_tok_cb2, L0_tok_sw3, L0_tok_cw3, L0_tok_cb3, L0_tok_fc1_w, L0_tok_fc1_b, L0_tok_fc2_w, L0_tok_fc2_b, L0_attn_Wq, L0_attn_bq, L0_attn_Wk, L0_attn_bk, L0_attn_Wv, L0_attn_bv, L0_attn_Wo, L0_attn_bo, L0_ffn_gate_w, L0_ffn_gate_b, L0_ffn_w1, L0_ffn_b1, L0_ffn_w2, L0_ffn_b2, L0_ffn_gamma, L0_ffn_beta):
    import jax
    import jax.numpy as jnp

    def _L0_tok_ref(coords, fc0_w, fc0_b, sw0, cw0, cb0, sw1, cw1, cb1, sw2, cw2, cb2, sw3, cw3, cb3, fc1_w, fc1_b, fc2_w, fc2_b):
        import jax, jax.numpy as jnp
        import numpy as np
        M1 = 20
        M2 = 20

        def _spectral_conv(x, w):
            B, Cin, H, W = x.shape
            x_ft = jnp.fft.rfft2(x, norm='ortho')
            out = jnp.einsum('bixy,ioxy->boxy', x_ft[:, :, :M1, :M2], w.astype(x_ft.dtype))
            out_ft = jnp.zeros((B, w.shape[1], H, W // 2 + 1), dtype=x_ft.dtype)
            out_ft = out_ft.at[:, :, :M1, :M2].set(out)
            return jnp.fft.irfft2(out_ft, s=(H, W), norm='ortho')

        def _gelu(x):
            return jax.nn.gelu(x, approximate=False)
        x = coords @ fc0_w + fc0_b
        x = jnp.transpose(x, (0, 3, 1, 2))
        for sw, cw, cb in ((sw0, cw0, cb0), (sw1, cw1, cb1), (sw2, cw2, cb2), (sw3, cw3, cb3)):
            x1 = _spectral_conv(x, sw)
            x2 = jnp.einsum('bchw,oc->bohw', x, cw) + cb[None, :, None, None]
            x = _gelu(x1 + x2)
        x = jnp.transpose(x, (0, 2, 3, 1))
        x = _gelu(x @ fc1_w + fc1_b)
        return (x @ fc2_w + fc2_b)[..., 0]

    def _L0_attn_ref(src, Wq, bq, Wk, bk, Wv, bv, Wo, bo):
        import jax, jax.numpy as jnp
        import numpy as np
        import math
        B, S, D = (4, 1024, 64)
        q = src @ Wq.T + bq
        k = src @ Wk.T + bk
        v = src @ Wv.T + bv
        row_mask = (q[:, :, 0] != 0) & (k[:, :, 0] != 0)
        mask = row_mask[:, :, None]
        scale = 1.0 / math.sqrt(D)
        scores = jnp.einsum('bid,bjd->bij', q, k) * scale
        scores = jnp.where(mask, scores, jnp.float32(-1000000000.0))
        prob = jax.nn.softmax(scores, axis=-1)
        prob = jnp.where(mask, prob, 0.0)
        out = jnp.einsum('bij,bjd->bid', prob, v)
        return out @ Wo.T + bo

    def _L0_ffn_ref(x, gate_w, gate_b, w1, b1, w2, b2, gamma, beta):
        import jax, jax.numpy as jnp
        import numpy as np
        B, S, H, F, E, K = (8, 1024, 64, 128, 16, 2)
        EPS = 1e-05
        gate_logits = x @ gate_w + gate_b
        topk_vals, topk_idx = jax.lax.top_k(gate_logits, K)
        topk_w = jax.nn.softmax(topk_vals, axis=-1)
        h = jax.nn.relu(jnp.einsum('bsh,ehf->bsef', x, w1) + b1)
        expert_out = jnp.einsum('bsef,efh->bseh', h, w2) + b2
        sel = jnp.take_along_axis(expert_out, topk_idx[:, :, :, None], axis=2)
        moe = jnp.sum(topk_w[..., None] * sel, axis=2)
        y = x + moe
        mu = jnp.mean(y, axis=-1, keepdims=True)
        var = jnp.var(y, axis=-1, keepdims=True)
        return (y - mu) / jnp.sqrt(var + EPS) * gamma + beta
    h = _L0_tok_ref(x, L0_tok_fc0_w, L0_tok_fc0_b, L0_tok_sw0, L0_tok_cw0, L0_tok_cb0, L0_tok_sw1, L0_tok_cw1, L0_tok_cb1, L0_tok_sw2, L0_tok_cw2, L0_tok_cb2, L0_tok_sw3, L0_tok_cw3, L0_tok_cb3, L0_tok_fc1_w, L0_tok_fc1_b, L0_tok_fc2_w, L0_tok_fc2_b)
    h = h + _L0_attn_ref(_layernorm(h, axis=-1), L0_attn_Wq, L0_attn_bq, L0_attn_Wk, L0_attn_bk, L0_attn_Wv, L0_attn_bv, L0_attn_Wo, L0_attn_bo)
    h = h + _L0_ffn_ref(_layernorm(h, axis=-1), L0_ffn_gate_w, L0_ffn_gate_b, L0_ffn_w1, L0_ffn_b1, L0_ffn_w2, L0_ffn_b2, L0_ffn_gamma, L0_ffn_beta)
    return h

_drawn_inputs = setup_inputs


def setup_inputs(seed=0):
    import zlib

    import numpy as np

    out = dict(_drawn_inputs(seed))
    spreads = {'L0_tok_fc0_b': (0.0, 0.8),
     'L0_tok_cb0': (0.0, 0.8),
     'L0_tok_cb1': (0.0, 0.8),
     'L0_tok_cb2': (0.0, 0.8),
     'L0_tok_cb3': (0.0, 0.8),
     'L0_tok_fc1_b': (0.0, 0.751),
     'L0_ffn_gate_b': (0.0, 0.1),
     'L0_ffn_b1': (0.0, 0.8),
     'L0_ffn_b2': (0.0, 0.1),
     'L0_ffn_gamma': (1.0, 0.2),
     'L0_ffn_beta': (0.0, 0.1)}
    factors = {'L0_tok_sw0': 8.0,
     'L0_tok_sw1': 8.0,
     'L0_tok_sw2': 8.0,
     'L0_tok_sw3': 8.0,
     'L0_tok_fc2_w': 4.018,
     'L0_attn_Wq': 8.0,
     'L0_attn_bq': 8.0,
     'L0_attn_Wk': 8.0,
     'L0_attn_bk': 8.0,
     'L0_ffn_w1': 5.112,
     'L0_ffn_w2': 3.799}
    for name, (base, spread) in spreads.items():
        noise = np.random.default_rng([zlib.crc32(name.encode()), seed]).standard_normal(out[name].shape)
        drawn = base * np.exp(spread * noise) if base else spread * noise
        out[name] = jnp.asarray(drawn.astype(out[name].dtype))
    for name, factor in factors.items():
        out[name] = (out[name] * factor).astype(out[name].dtype)
    return out
```

```python
import numpy as np
import concourse.bass as bass
from concourse import mybir
from contextlib import ExitStack

IMAGES, H, W, C, MODES, LAYERS = 64, 64, 64, 32, 20, 4
GROUPS = 2
GI = IMAGES // GROUPS
WL = W // 2
KH4, KHH = 4, MODES // 4
KHP = 32
SPEC = KHH * MODES * 2
MIXN = 10
MIXS = KHH * MODES // MIXN
MF = MIXN * 2 * GI
F1F = 64
TOK, D, E, F = IMAGES * H, 64, 16, 128
CH = 512
CT = CH // 128
EPS = 1e-5


assert GROUPS <= 2


def dft_constants():
    k, w, h = np.arange(MODES), np.arange(W), np.arange(H)
    ang_w = 2 * np.pi * np.outer(w, k) / W
    ang_h = 2 * np.pi * np.outer(h, k) / H
    cw, sw, chh, shh = np.cos(ang_w), np.sin(ang_w), np.cos(ang_h), np.sin(ang_h)
    fh = np.zeros((2, H, 2, 2, KHP))
    ih = np.zeros((2, 2, KHP, 2, H))
    for a in range(2):
        fh[a, :, a, 0, :MODES], fh[a, :, a, 1, :MODES] = chh, -shh
        ih[a, 0, :MODES, a, :], ih[a, 1, :MODES, a, :] = chh.T, -shh.T
    fw = np.zeros((2, 2, WL, MODES, 2))
    iw = np.zeros((128, 2, 2, WL))
    twice = np.where(k == 0, 1.0, 2.0)[:, None]
    for a in range(2):
        c, s = cw[a * WL:(a + 1) * WL], sw[a * WL:(a + 1) * WL]
        fw[a, 0, :, :, 0], fw[a, 1, :, :, 0] = c, s
        fw[a, 0, :, :, 1], fw[a, 1, :, :, 1] = -s, c
        iw[0:2 * MODES:2, a, 0], iw[1:2 * MODES:2, a, 0] = twice * c.T, -twice * s.T
        iw[0:2 * MODES:2, a, 1], iw[1:2 * MODES:2, a, 1] = twice * s.T, twice * c.T
    parts = [fh.reshape(128, 128), ih.reshape(128, 128), iw.reshape(128, 128), np.eye(128), fw.reshape(128, 40)]
    return (np.concatenate(parts, 1) * np.array([0.125] * 384 + [1.0] * 128 + [0.125] * 40)).astype(np.float32)


def vit_tower(nc, x, dft, mix_w, conv_w, conv_b, fc0_w, fc1_w, fc1_b, fc2_w, fc2_b,
              attn_w, moe_w1, moe_w2, gate_w, moe_b2, ln_gb, out, h_dram):
    f32, u32 = mybir.dt.float32, mybir.dt.uint32
    ALU, ACT, AX = mybir.AluOpType, mybir.ActivationFunctionType, mybir.AxisListType
    ds = bass.ds

    with ExitStack() as ctx:
        def sb(name, shape, dt=f32):
            return ctx.enter_context(nc.sbuf_tensor(name, shape, dt))

        def sem(name):
            return ctx.enter_context(nc.semaphore(name))

        stored_b = sb("stored_b", [128, GI, 1024])
        spec = sb("spec", [128, KHH * MODES, 2, GI])
        mix_slot = [sb(f"mix_slot{u}", [128, MIXN, 128]) for u in range(2)]
        stage_b = [sb(f"stage_b{u}", [128, 8, 128]) for u in range(2)]
        stage_t = [sb(f"stage_t{u}", [128, KHH, 40]) for u in range(2)]
        pix = sb("pix", [128, 8, C, 4])
        y_sb = sb("y_sb", [128, KHP, C])
        u_sb = sb("u_sb", [128, 8, C, 4])
        tt_sb = sb("tt_sb", [128, MODES, C])
        consts = sb("consts", [128, 552])
        fwd_h, inv_h, inv_w = consts[:, 0:128], consts[:, 128:256], consts[:, 256:384]
        ident, fwd_w = consts[:, 384:512], consts[:, 512:552]
        conv_sb = sb("conv_sb", [128, LAYERS, 128])
        convb_raw = sb("convb_raw", [C, LAYERS])
        convb_sb = sb("convb_sb", [C, LAYERS])
        x_in = [sb(f"x_in{u}", [128, 96]) for u in range(2)]
        xt_sb = sb("xt_sb", [97, 128])
        fc0_sb = sb("fc0_sb", [97, 1024])
        fc1_sb = sb("fc1_sb", [128, 2, 128])
        fc1b_sb = sb("fc1b_sb", [128, 1])
        fc2_sb = sb("fc2_sb", [128, 2])
        fc2b_sb = sb("fc2b_sb", [128, 1])
        h_sb = sb("h_sb", [128, GI, WL])
        b_last = y_sb[:, :, :].rearrange("p a b -> p (a b)")
        g_sb = sb("g_sb", [128, 2, 512])

        ps = ctx.enter_context(nc.psum_tensor("ps", [128, 8, 512], f32))
        x_ps, y_ps, u_ps, t_ps = ps[:, 0:2], ps[:, 2:4], ps[:, 4:6], ps[:, 6:8]
        s_ps = ps[:, 2, 0:SPEC]

        pool = stored_b[:, :, :].rearrange("p a b -> p (a b)")
        at = [0]

        def take(parts, *shape):
            n = int(np.prod(shape))
            v = pool[0:parts, at[0]:at[0] + n]
            at[0] += n
            names = "abc"[:len(shape)]
            if len(shape) > 1:
                v = v.rearrange(f"p ({' '.join(names)}) -> p {' '.join(names)}", **dict(zip(names, shape)))
            return v

        tok_h = take(128, CT, D)
        tok_c = take(128, CT, D)
        tok_q = take(128, CT, D)
        tok_n = take(128, CT, D)
        xt = take(65, CH)
        q_t = take(64, CH)
        k_t = take(64, CH)
        v_sb = take(128, CT, D + 2)
        score = take(128, CT, D)
        prob_bd = take(128, CT, 128)
        prob_t = take(128, CT, 128)
        o_t = take(65, CH)
        tok_h2 = take(128, CT, D)
        tok_n2 = take(128, CT, D)
        logit = take(128, CT, E)
        oh1 = take(128, CT, E)
        oh2 = take(128, CT, E)
        gate = take(128, CT, E)
        gate_t = take(16, CH)
        relu = [take(128, CH) for _ in range(2)]
        weighed = take(128, CT, D)
        acc = take(128, CT, D)
        tok_o = take(128, CT, D)
        stat = take(128, 16, CT)
        top8 = take(128, CT, 8)
        idx_f = take(128, CT, 8)
        iota_f = take(128, E)
        attn_sb = take(65, 3 * D + 2 + D)
        w1_sb = take(65, E, F)
        w2_sb = take(128, E, D)
        gate_sb = take(65, E)
        b2_sb = take(16, D)
        gb_sb = take(128, 2, D)
        idx_u = sb("idx_u", [128, CT, 8], u32)
        iota_u = sb("iota_u", [128, E], mybir.dt.int32)

        ld_const = sem("ld_const")
        init_done = sem("init_done")
        ld_x = [sem(f"ld_x{u}") for u in range(2)]
        ld_mix = [sem(f"ld_mix{u}") for u in range(2)]
        pe_xt, pe_x, pe_bt, pe_y, pe_s = sem("pe_xt"), sem("pe_x"), sem("pe_bt"), sem("pe_y"), sem("pe_s")
        pe_tt, pe_u, pe_mix, pe_fc1, pe_fc2 = sem("pe_tt"), sem("pe_u"), sem("pe_mix"), sem("pe_fc1"), sem("pe_fc2")
        act_pix, act_b, act_mix, act_g = sem("act_pix"), sem("act_b"), sem("act_mix"), sem("act_g")
        dve_xt, dve_tt, dve_u, dve_y = sem("dve_xt"), sem("dve_tt"), sem("dve_u"), sem("dve_y")
        dve_s, dve_mix, dve_cb, dve_h = sem("dve_s"), sem("dve_mix"), sem("dve_cb"), sem("dve_h")
        pool_st = sem("pool_st")
        st_h = sem("st_h")
        ld_tail, ld_tok, st_out = sem("ld_tail"), sem("ld_tok"), sem("st_out")
        tail_init = sem("tail_init")
        t_pe, t_act, t_dve = sem("t_pe"), sem("t_act"), sem("t_dve")
        t_h1, t_relu, t_eo, t_acc = sem("t_h1"), sem("t_relu"), sem("t_eo"), sem("t_acc")

        counted = [pe_xt, pe_x, pe_bt, pe_y, pe_s, pe_tt, pe_u, pe_mix, pe_fc1, pe_fc2, act_pix, act_b, act_mix, act_g,
                   dve_xt, dve_tt, dve_u, dve_y, dve_s, dve_mix, dve_cb, dve_h, pool_st, st_h, st_out]

        passed = sem("passed")

        def after(eng, s, n):
            eng.wait_ge(s, n + 1)

        block = ctx.enter_context(nc.Block())

        def image_loop(eng, body):
            body(0, 0, True, False)
            with eng.Fori(0, (GI - 2) // 2) as p:
                for k in range(2):
                    body(p * 2 + (1 + k), (1 + k) % 2, False, False)
            body(GI - 1, (GI - 1) % 2, False, True)

        NCONST = 9

        @block.sync
        def _(sp):
            for s in counted:
                sp.sem_inc(s, 1)
            for dst, src in ((consts[:, :], dft), (fc0_sb[:, :], fc0_w), (conv_sb[:, :, :], conv_w),
                             (convb_raw[:, :], conv_b), (fc1_sb[:, :, :], fc1_w), (fc1b_sb[:, :], fc1_b),
                             (fc2_sb[:, :], fc2_w), (fc2b_sb[:, :], fc2_b.to_broadcast([128, 1]))):
                sp.dma_start(dst, src).then_inc(ld_const, 16)

            def load_x(g, i, u, free):
                after(sp, pe_xt, free)
                sp.dma_start(x_in[u][:, :], x[ds(g * GI + i, 1)].rearrange("b p f -> p (b f)")).then_inc(ld_x[u], 16)

            def load_mix(s, u, free):
                after(sp, pe_mix, free)
                sp.dma_start(mix_slot[u][:, :, :].rearrange("p m o -> p (m o)"),
                             mix_w[ds(s, 1)].rearrange("s p f -> p (s f)")).then_inc(ld_mix[u], 16)

            with sp.Fori(0, GROUPS) as g:
                load_x(g, 0, 0, g * GI)
                load_x(g, 1, 1, g * GI)
                with sp.Fori(0, GI // 2 - 1) as p:
                    for u in range(2):
                        load_x(g, p * 2 + 2 + u, u, g * GI + p * 2 + u + 1)
                steps = LAYERS * MIXS
                load_mix(0, 0, g * (steps - 1))
                load_mix(1, 1, g * steps)
                with sp.Fori(0, steps // 2 - 1) as p:
                    for u in range(2):
                        load_mix(p * 2 + 2 + u, u, g * steps + p * 2 + 1 + u)
                after(sp, dve_h, g * GI + GI)
                for w_hi in range(2):
                    sp.dma_start(h_dram[ds(g * GI, GI), :, w_hi * WL:(w_hi + 1) * WL].rearrange("b h w -> h b w"),
                                 h_sb[w_hi * H:(w_hi + 1) * H, :, :]).then_inc(st_h, 16)
            after(sp, st_h, 32 * GROUPS)
            after(sp, pool_st, 2 * IMAGES * LAYERS)
            after(sp, pe_fc2, 4 * IMAGES)
            for dst, src in ((attn_sb, attn_w), (w1_sb, moe_w1), (w2_sb, moe_w2), (gate_sb, gate_w), (b2_sb, moe_b2),
                             (gb_sb, ln_gb.rearrange("(o a) d -> o a d", o=1).to_broadcast([128, 2, D]))):
                sp.dma_start(dst, src).then_inc(ld_tail, 16)
            rows = h_dram.rearrange("b (q h) w -> (b q h) w", q=1).rearrange("(c t p) w -> c p t w", t=CT, p=128)
            out_rows = out.rearrange("b h w -> (b h) w").rearrange("(c t p) w -> c p t w", t=CT, p=128)
            with sp.Fori(0, TOK // CH) as c:
                after(sp, st_out, c * 16)
                sp.dma_start(tok_h, rows[ds(c, 1)].rearrange("c p t w -> p (c t) w")).then_inc(ld_tok, 16)
                sp.wait_ge(t_dve, TAIL["dve"] * (c + 1))
                sp.dma_start(out_rows[ds(c, 1)].rearrange("c p t w -> p (c t) w"), tok_o).then_inc(st_out, 16)
            after(sp, st_out, 16 * (TOK // CH))

        @block.gpsimd
        def _(gp):
            gp.iota(iota_u[:, :], pattern=[[1, E]], base=0, channel_multiplier=0).then_inc(init_done, 1)
            gp.memset(tt_sb[:, :, :], 0.0).then_inc(init_done, 1)
            gp.memset(xt_sb[:, :], 1.0).then_inc(init_done, 1)
            with gp.Fori(0, GROUPS) as g:
                with gp.Fori(0, LAYERS) as layer:
                    base = (g * LAYERS + layer) * GI
                    steps = (g * LAYERS + layer + 1) * (MIXS // 2)
                    after(gp, dve_mix, steps)
                    after(gp, act_mix, steps)
                    after(gp, dve_cb, g * LAYERS + layer + 2)

                    def stage(i, u, reads):
                        if reads is not None:
                            after(gp, pe_x, reads)
                        gp.sem_inc(passed, 1)
                        gp.tensor_copy(stage_b[u][:, :, :].rearrange("p a b -> p (a b)"),
                                       stored_b[:, ds(i, 1), :].rearrange("p a b -> p (a b)")).then_inc(pool_st, 1)
                        gp.tensor_copy(stage_t[u][:, :, :].rearrange("p a b -> p (a b)"),
                                       spec[:, :, :, ds(i, 1)].rearrange("p a b c -> p (a b c)")).then_inc(pool_st, 1)
                    xbase = (g * (LAYERS + 1) + layer + 1) * GI
                    stage(0, 0, None)
                    stage(1, 1, None)
                    with gp.Fori(0, GI // 2 - 1) as p:
                        for u in range(2):
                            stage(p * 2 + 2 + u, u, xbase + p * 2 + u + 1)
            gp.wait_ge(t_dve, 1)

        @block.tensor
        def _(pe):
            mm = pe.matmul
            a_flat = pix[:, :, :, :].rearrange("p (a b) c w -> p a (b c w)", a=2)
            pe.wait_ge(ld_const, 16 * (NCONST - 1))
            pe.wait_ge(init_done, 4)

            def transpose_pixels(n):
                after(pe, act_pix, n + 1)
                for b in range(8):
                    src = pix[:, b, :, :].rearrange("p c w -> p (c w)")
                    last = pe.transpose(t_ps[:, b // 4, (b % 4) * 128:(b % 4 + 1) * 128], src, ident)
                last.then_inc(pe_bt, 1)

            def forward_h(f):
                after(pe, dve_s, f)
                for a in range(2):
                    last = mm(y_ps[:, a, :], fwd_h, a_flat[:, a, :], start=True, stop=True)
                last.then_inc(pe_y, 1)

            def forward_w(f):
                after(pe, dve_y, f + 1)
                y = y_sb[:, :, :].rearrange("p k c -> p (k c)")
                for k in range(KHH):
                    last = mm(s_ps[:, k * 40:(k + 1) * 40], y[:, k * 128:(k + 1) * 128], fwd_w, start=True, stop=True)
                last.then_inc(pe_s, 1)

            def transpose_spec(v, u, n_before):
                after(pe, pool_st, 2 * v + 2)
                after(pe, act_b, n_before)
                pe.sem_inc(passed, 1)
                for k in range(KHH):
                    last = pe.transpose(t_ps[0:40, k // 4, (k % 4) * 128:(k % 4 + 1) * 128], stage_t[u][:, k, :], ident)
                last.then_inc(pe_tt, 1)

            def inverse_w(v):
                after(pe, dve_tt, v + 1)
                after(pe, dve_u, v)
                t = tt_sb[:, :, :].rearrange("p k o -> p (k o)")
                mm(u_ps[:, 0, :], inv_w, t[:, 0:512], start=True, stop=True)
                mm(u_ps[:, 1, 0:128], inv_w, t[:, 512:640], start=True, stop=True).then_inc(pe_u, 1)

            def conv_inverse_h(layer, u, v):
                after(pe, dve_u, v + 1)
                wc = conv_sb[:, ds(layer, 1), :].rearrange("p a b -> p (a b)")
                uf = u_sb[:, :, :, :].rearrange("p (a b) o w -> p a (b o w)", a=2)
                for a in range(2):
                    mm(x_ps[:, a, :], inv_h, uf[:, a, :], start=True, stop=False, skip_group_check=True)
                    for b in range(4):
                        last = mm(x_ps[:, a, b * 128:(b + 1) * 128], stage_b[u][:, a * 4 + b, :], wc, start=False, stop=(b == 3), skip_group_check=True)
                last.then_inc(pe_x, 1)

            def transpose_x(m, u, lds, n_before):
                pe.wait_ge(ld_x[u], lds)
                after(pe, act_b, n_before)
                pe.transpose(t_ps[0:96, 0, 0:128], x_in[u][:, :], ident).then_inc(pe_xt, 1)

            def lift(m):
                after(pe, dve_xt, m + 1)
                for a in range(2):
                    last = mm(x_ps[:, a, :], xt_sb[:, :], fc0_sb[:, a * 512:(a + 1) * 512], start=True, stop=True)
                last.then_inc(pe_x, 1)

            def mix(g, layer):
                gl = g * LAYERS + layer
                after(pe, dve_s, gl * GI + GI)
                after(pe, act_b, (g * (LAYERS + 1) + layer + 1) * GI)
                pe.sem_inc(passed, 1)
                with pe.Fori(0, MIXS // 2) as p:
                    for u, dst in ((0, x_ps), (1, t_ps)):
                        done = gl * (MIXS // 2) + p
                        pe.wait_ge(ld_mix[u], done * 16 + 16)
                        after(pe, (dve_mix, act_mix)[u], done)
                        for m in range(MIXN):
                            src = spec[:, ds((p * 2 + u) * MIXN + m, 1), :, :].rearrange("p a r i -> p (a r i)")
                            o = dst[:, m // 5, (m % 5) * 2 * GI:(m % 5 + 1) * 2 * GI]
                            last = mm(o, mix_slot[u][:, m, :], src, start=True, stop=True)
                        last.then_inc(pe_mix, 1)
                done = (gl + 1) * (MIXS // 2)
                after(pe, dve_mix, done)
                after(pe, act_mix, done)

            with pe.Fori(0, GROUPS) as g:
                nb = g * (LAYERS + 1) * GI
                transpose_x(g * GI, 0, g * (16 * GI // 2) + 16, nb)

                def first_pass(i, u, first, last):
                    m, n, f = g * GI + i, nb + i, g * LAYERS * GI + i
                    after(pe, act_pix, n)
                    lift(m)
                    if not last:
                        transpose_x(m + 1, 1 - u, g * (16 * GI // 2) + (i + u) * 8 + 16, n)
                    if not first:
                        forward_w(f - 1)
                    if not last:
                        after(pe, dve_xt, m + 2)
                    transpose_pixels(n)
                    forward_h(f)

                image_loop(pe, first_pass)
                forward_w(g * LAYERS * GI + GI - 1)

                with pe.Fori(0, LAYERS - 1) as layer:
                    mix(g, layer)
                    v0, n0, f0 = (g * LAYERS + layer) * GI, nb + (layer + 1) * GI, (g * LAYERS + layer + 1) * GI
                    transpose_spec(v0, 0, n0)
                    inverse_w(v0)

                    def layer_pass(i, u, first, last):
                        v, n, f = v0 + i, n0 + i, f0 + i
                        conv_inverse_h(layer, u, v)
                        if not last:
                            transpose_spec(v + 1, 1 - u, n)
                        if not first:
                            forward_w(f - 1)
                        if not last:
                            inverse_w(v + 1)
                        transpose_pixels(n)
                        forward_h(f)

                    image_loop(pe, layer_pass)
                    forward_w(f0 + GI - 1)

                mix(g, LAYERS - 1)
                v0, n0 = (g * LAYERS + LAYERS - 1) * GI, nb + LAYERS * GI
                transpose_spec(v0, 0, n0)
                inverse_w(v0)

                def last_pass(i, u, first, last):
                    v, n, m = v0 + i, n0 + i, g * GI + i
                    after(pe, dve_h, m)
                    conv_inverse_h(LAYERS - 1, u, v)
                    if not last:
                        transpose_spec(v + 1, 1 - u, n)
                        inverse_w(v + 1)
                    transpose_pixels(n)
                    after(pe, act_b, n + 1)

                    def fc1(c):
                        if c >= 2:
                            after(pe, act_g, m * 4 + c - 1)
                        mm(y_ps[:, c % 2, :], fc1_sb[:, c % 2, :], b_last[:, (c // 2) * 512:(c // 2 + 1) * 512],
                           start=True, stop=True).then_inc(pe_fc1, 1)

                    def fc2(c):
                        after(pe, act_g, m * 4 + c + 1)
                        for b in range(4):
                            w = (c // 2) * 16 + b * 4 + (c % 2) * 2
                            ins = mm(x_ps[:, 0, w:w + 2], g_sb[:, c % 2, b * 128:(b + 1) * 128], fc2_sb[:, :],
                                     start=True, stop=True, skip_group_check=True)
                        ins.then_inc(pe_fc2, 1)

                    fc1(0)
                    fc1(1)
                    fc2(0)
                    fc1(2)
                    fc2(1)
                    fc1(3)
                    fc2(2)
                    fc2(3)

                image_loop(pe, last_pass)
                after(pe, dve_h, g * GI + GI)

            pe.wait_ge(ld_tail, 16 * 6)
            pe.wait_ge(tail_init, 4)
            b0, b1, b2, b3, b4, b5, b6, b7 = (ps[:, k, :] for k in range(8))
            with pe.Fori(0, TOK // CH) as c:
                def when(s, k, total):
                    pe.wait_ge(s, c * total + k)
                nd, na = TAIL["dve"], TAIL["act"]
                when(t_dve, TAIL["d_n1"], nd)
                pe.sem_inc(passed, 1)
                for t in range(CT):
                    last = pe.transpose(b0[0:64, t * 128:(t + 1) * 128], tok_n[:, t, :], ident)
                last.then_inc(t_pe, 1)
                when(t_act, 2, na)
                mm(b1[0:64, :], attn_sb[:, 0:64], xt, start=True, stop=True).then_inc(t_pe, 1)
                mm(b2[0:64, :], attn_sb[:, 64:128], xt, start=True, stop=True).then_inc(t_pe, 1)
                for t in range(CT):
                    last = mm(b3[:, t * 66:(t + 1) * 66], xt[:, t * 128:(t + 1) * 128], attn_sb[:, 128:194],
                              start=True, stop=True, skip_group_check=True)
                last.then_inc(t_pe, 1)
                when(t_act, 3, na)
                when(t_dve, TAIL["d_k"], nd)
                pe.sem_inc(passed, 1)
                for t in range(CT):
                    for b in range(2):
                        tk = slice(t * 128 + b * 64, t * 128 + b * 64 + 64)
                        last = mm(b4[b * 64:(b + 1) * 64, t * 64:(t + 1) * 64], q_t[:, tk], k_t[:, tk],
                                  start=True, stop=True, skip_group_check=True)
                last.then_inc(t_pe, 1)
                when(t_dve, TAIL["d_p"], nd)
                for t in range(CT):
                    last = pe.transpose(b5[:, t * 128:(t + 1) * 128], prob_bd[:, t, :], ident)
                last.then_inc(t_pe, 1)
                when(t_act, 5, na)
                for t in range(CT):
                    last = mm(b6[0:64, t * 128:(t + 1) * 128], v_sb[:, t, 0:64], prob_t[:, t, :],
                              start=True, stop=True, skip_group_check=True)
                last.then_inc(t_pe, 1)
                when(t_dve, TAIL["d_o"], nd)
                for t in range(CT):
                    last = mm(b7[:, t * 64:(t + 1) * 64], o_t[:, t * 128:(t + 1) * 128], attn_sb[:, 194:258],
                              start=True, stop=True, skip_group_check=True)
                last.then_inc(t_pe, 1)
                when(t_dve, TAIL["d_n2"], nd)
                pe.sem_inc(passed, 1)
                for t in range(CT):
                    last = pe.transpose(b0[0:64, t * 128:(t + 1) * 128], tok_n2[:, t, :], ident)
                last.then_inc(t_pe, 1)
                when(t_act, 7, na)
                for t in range(CT):
                    last = mm(b1[:, t * E:(t + 1) * E], xt[:, t * 128:(t + 1) * 128], gate_sb[:, :],
                              start=True, stop=True, skip_group_check=True)
                last.then_inc(t_pe, 1)
                when(t_dve, TAIL["d_g"], nd)
                for t in range(CT):
                    last = pe.transpose(b2[0:16, t * 128:(t + 1) * 128], gate[:, t, :], ident)
                last.then_inc(t_pe, 1)
                when(t_act, 9, na)
                for t in range(CT):
                    last = mm(b3[:, t * 64:(t + 1) * 64], gate_t[:, t * 128:(t + 1) * 128], b2_sb[:, :],
                              start=True, stop=True, skip_group_check=True)
                last.then_inc(t_pe, 1)

                def up(e):
                    if e >= 2:
                        pe.wait_ge(t_relu, c * E + e - 1)
                    mm(ps[:, 4 + e % 2, :], w1_sb[:, e, :], xt, start=True, stop=True).then_inc(t_h1, 1)

                def down(e):
                    pe.wait_ge(t_relu, c * E + e + 1)
                    if e >= 2:
                        pe.wait_ge(t_acc, c * E + e - 1)
                    for t in range(CT):
                        last = mm(ps[:, 6 + e % 2, t * 64:(t + 1) * 64], relu[e % 2][:, t * 128:(t + 1) * 128],
                                  w2_sb[:, e, :], start=True, stop=True, skip_group_check=True)
                    last.then_inc(t_eo, 1)

                up(0)
                for e in range(E):
                    if e + 1 < E:
                        up(e + 1)
                    down(e)

        @block.scalar
        def _(act):
            pix_f = pix[:, :, :, :].rearrange("p a c w -> p (a c w)")
            x_f = x_ps.rearrange("p a b -> p (a b)")
            t_f = t_ps.rearrange("p a b -> p (a b)")

            def to_pixels(n, func):
                after(act, pe_x, n + 1)
                after(act, pe_bt, n)
                act.activation(pix_f, x_f, func).then_inc(act_pix, 1)

            def store_b(n, dst):
                after(act, pe_bt, n + 1)
                act.activation(dst, t_f, ACT.Copy).then_inc(act_b, 1)

            with act.Fori(0, GROUPS) as g:
                nb = g * (LAYERS + 1) * GI

                def stored(i):
                    return stored_b[:, ds(i, 1), :].rearrange("p a b -> p (a b)")

                def first_pass(i, u, first, last):
                    after(act, pe_y, g * LAYERS * GI + i)
                    to_pixels(nb + i, ACT.Copy)
                    store_b(nb + i, stored(i))

                image_loop(act, first_pass)

                def mix_evac(layer):
                    with act.Fori(0, MIXS // 2) as p:
                        gl = g * LAYERS + layer
                        after(act, pe_mix, gl * MIXS + p * 2 + 2)
                        dst = spec[:, ds((p * 2 + 1) * MIXN, MIXN), :, :].rearrange("p (b m) r i -> p b (m r i)", b=2)
                        act.activation(dst, t_ps[:, :, 0:MF // 2], ACT.Copy).then_inc(act_mix, 1)

                with act.Fori(0, LAYERS - 1) as layer:
                    mix_evac(layer)

                    def layer_pass(i, u, first, last):
                        after(act, pe_y, (g * LAYERS + layer + 1) * GI + i)
                        to_pixels(nb + (layer + 1) * GI + i, ACT.Gelu)
                        store_b(nb + (layer + 1) * GI + i, stored(i))

                    image_loop(act, layer_pass)
                mix_evac(LAYERS - 1)

                def last_pass(i, u, first, last):
                    n, m = nb + LAYERS * GI + i, g * GI + i
                    to_pixels(n, ACT.Gelu)
                    after(act, pe_fc1, m * 4)
                    store_b(n, b_last)
                    for c in range(4):
                        after(act, pe_fc1, m * 4 + c + 1)
                        after(act, pe_fc2, m * 4 + c - 1 if c >= 2 else m * 4)
                        act.activation(g_sb[:, c % 2, :], y_ps[:, c % 2, :], ACT.Gelu, bias=fc1b_sb[:, :]).then_inc(act_g, 1)

                image_loop(act, last_pass)

            with act.Fori(0, TOK // CH) as c:
                def when(s, k, total):
                    act.wait_ge(s, c * total + k)
                npe, nd = TAIL["pe"], TAIL["dve"]

                def root(k):
                    when(t_dve, TAIL[f"d_v{k}"], nd)
                    act.activation(stat[:, 4, :], stat[:, 3, :], ACT.Sqrt).then_inc(t_act, 1)

                root(1)
                when(t_pe, 1, npe)
                act.activation(xt[0:64, :], ps[0:64, 0, :], ACT.Copy).then_inc(t_act, 1)
                when(t_pe, 2, npe)
                act.activation(q_t, ps[0:64, 1, :], ACT.Copy).then_inc(t_act, 1)
                when(t_dve, TAIL["d_sub"], nd)
                act.activation(score, score, ACT.Exp, scale=float(D) ** -0.5).then_inc(t_act, 1)
                when(t_pe, 6, npe)
                act.activation(prob_t, ps[:, 5, :].rearrange("p (t j) -> p t j", t=CT), ACT.Copy).then_inc(t_act, 1)
                root(6)
                when(t_pe, 9, npe)
                act.activation(xt[0:64, :], ps[0:64, 0, :], ACT.Copy).then_inc(t_act, 1)
                when(t_dve, TAIL["d_dv"], nd)
                act.activation(stat[:, 8, :], stat[:, 7, :], ACT.Exp).then_inc(t_act, 1)
                when(t_pe, 11, npe)
                act.activation(gate_t, ps[0:16, 2, :], ACT.Copy).then_inc(t_act, 1)
                for e in range(E):
                    act.wait_ge(t_h1, c * E + e + 1)
                    if e >= 2:
                        act.wait_ge(t_eo, c * E + e - 1)
                    act.activation(relu[e % 2], ps[:, 4 + e % 2, :], ACT.Relu).then_inc(t_relu, 1)
                root(10)

        @block.vector
        def _(dve):
            dve.memset(u_ps, 0.0).then_inc(init_done, 1)
            dve.wait_ge(ld_const, 16 * (NCONST - 1))
            dve.tensor_scalar(convb_sb[:, :], convb_raw[:, :], float(H * W) ** 0.5, None, ALU.mult).then_inc(dve_cb, 1)
            after(dve, dve_cb, 1)
            dve.wait_ge(init_done, 4)

            def copy_tt(v):
                after(dve, pe_tt, v + 1)
                after(dve, pe_u, v)
                dve.tensor_copy(tt_sb[0:40, :, :].rearrange("p k o -> p (k o)"),
                                t_ps[0:40].rearrange("p a b -> p (a b)")[:, 0:640]).then_inc(dve_tt, 1)

            def turn_u(v, n):
                after(dve, pe_u, v + 1)
                after(dve, pe_x, n)
                src = u_ps.rearrange("p a (k o) -> p o (a k)", o=C)
                dve.transpose(u_sb[:, :, :, :].rearrange("p b o w -> p o b w"), src).then_inc(dve_u, 1)

            def turn_y(f):
                after(dve, pe_y, f + 1)
                after(dve, pe_s, f)
                src = y_ps.rearrange("p a (b c w) -> p c (a b) w", b=4, w=4)
                dve.transpose(y_sb[:, :, :].rearrange("p k c -> p c k"), src).then_inc(dve_y, 1)

            def keep_spec(f, i):
                after(dve, pe_s, f + 1)
                dve.tensor_copy(spec[:, :, :, ds(i, 1)].rearrange("p a b c -> p (a b c)"), s_ps).then_inc(dve_s, 1)

            with dve.Fori(0, GROUPS) as g:
                nb = g * (LAYERS + 1) * GI

                def copy_xt(m, n):
                    after(dve, pe_xt, m + 1)
                    after(dve, pe_x, n)
                    dve.tensor_copy(xt_sb[0:96, :], t_ps[0:96, 0, 0:128]).then_inc(dve_xt, 1)

                copy_xt(g * GI, nb)

                def first_pass(i, u, first, last):
                    m, f = g * GI + i, g * LAYERS * GI + i
                    if not last:
                        copy_xt(m + 1, nb + i + 1)
                    if not first:
                        keep_spec(f - 1, i - 1)
                    turn_y(f)

                image_loop(dve, first_pass)
                keep_spec(g * LAYERS * GI + GI - 1, GI - 1)

                def mix_evac(layer):
                    gl = g * LAYERS + layer
                    with dve.Fori(0, MIXS // 2) as p:
                        after(dve, pe_mix, gl * MIXS + p * 2 + 1)
                        dst = spec[:, ds((p * 2) * MIXN, MIXN), :, :].rearrange("p (b m) r i -> p b (m r i)", b=2)
                        dve.tensor_copy(dst, x_ps[:, :, 0:MF // 2]).then_inc(dve_mix, 1)
                    after(dve, dve_mix, (gl + 1) * (MIXS // 2))
                    mode0 = spec[0:C, 0, 0, :]
                    dve.tensor_tensor(mode0, mode0, convb_sb[:, ds(layer, 1)].to_broadcast([C, GI]), ALU.add).then_inc(dve_cb, 1)

                with dve.Fori(0, LAYERS - 1) as layer:
                    mix_evac(layer)
                    v0, n0, f0 = (g * LAYERS + layer) * GI, nb + (layer + 1) * GI, (g * LAYERS + layer + 1) * GI
                    copy_tt(v0)
                    turn_u(v0, n0)

                    def layer_pass(i, u, first, last):
                        if not last:
                            copy_tt(v0 + i + 1)
                        if not first:
                            keep_spec(f0 + i - 1, i - 1)
                        if not last:
                            turn_u(v0 + i + 1, n0 + i + 1)
                        turn_y(f0 + i)

                    image_loop(dve, layer_pass)
                    keep_spec(f0 + GI - 1, GI - 1)

                mix_evac(LAYERS - 1)
                v0, n0 = (g * LAYERS + LAYERS - 1) * GI, nb + LAYERS * GI
                copy_tt(v0)
                turn_u(v0, n0)
                after(dve, st_h, g * 32)

                def last_pass(i, u, first, last):
                    if not last:
                        copy_tt(v0 + i + 1)
                        turn_u(v0 + i + 1, n0 + i + 1)
                    after(dve, pe_fc2, (g * GI + i + 1) * 4)
                    dve.tensor_scalar(h_sb[:, ds(i, 1), :].rearrange("p a b -> p (a b)"), x_ps[:, 0, 0:WL],
                                      fc2b_sb[:, :], None, ALU.add).then_inc(dve_h, 1)

                image_loop(dve, last_pass)

            dve.wait_ge(ld_tail, 16 * 6)
            dve.memset(prob_bd, 0.0).then_inc(tail_init, 1)
            dve.memset(xt[64:65, :], 1.0).then_inc(tail_init, 1)
            dve.memset(o_t[64:65, :], 1.0).then_inc(tail_init, 1)
            dve.tensor_copy(iota_f, iota_u[:, :]).then_inc(tail_init, 1)
            dve.wait_ge(tail_init, 4)
            with dve.Fori(0, TOK // CH) as c:
                nd, npe, na = TAIL["dve"], TAIL["pe"], TAIL["act"]
                count = [0]

                def step(ins, mark=None, alone=False):
                    count[0] += 1
                    ins.then_inc(t_dve, 1)
                    if mark:
                        SEEN[mark] = count[0]
                    dve.wait_ge(t_dve, c * nd + count[0])
                    if alone:
                        dve.sem_inc(passed, 1)

                def when(s, k, total):
                    dve.wait_ge(s, c * total + k)

                def row(k):
                    return stat[:, k, :]

                def wide(v, n=D):
                    return v.unsqueeze(2).to_broadcast([128, CT, n])

                def norm(dst, src, root, mark=None):
                    step(dve.tensor_reduce(row(0), src, AX.X, ALU.add))
                    step(dve.tensor_scalar(row(1), row(0), 1.0 / D, None, ALU.mult))
                    step(dve.tensor_tensor(tok_c, src, wide(row(1)), ALU.subtract))
                    step(dve.tensor_tensor(tok_q, tok_c, tok_c, ALU.mult))
                    step(dve.tensor_reduce(row(2), tok_q, AX.X, ALU.add))
                    step(dve.tensor_scalar(row(3), row(2), 1.0 / D, EPS, ALU.mult, ALU.add), f"d_v{root}")
                    when(t_act, root, na)
                    step(dve.reciprocal(row(12), row(4)))
                    step(dve.tensor_tensor(dst, tok_c, wide(row(12)), ALU.mult), mark)

                dve.wait_ge(ld_tok, c * 16 + 16)
                norm(tok_n, tok_h, 1, "d_n1")
                when(t_pe, 3, npe)
                step(dve.tensor_copy(k_t, ps[0:64, 2, :]), "d_k")
                when(t_pe, 4, npe)
                step(dve.tensor_copy(v_sb, ps[:, 3, 0:CT * 66].rearrange("p (t d) -> p t d", t=CT)))
                step(dve.tensor_scalar(row(5), v_sb[:, :, 64], 0.0, None, ALU.not_equal))
                step(dve.tensor_scalar(row(6), v_sb[:, :, 65], 0.0, None, ALU.not_equal))
                step(dve.tensor_tensor(row(5), row(5), row(6), ALU.mult))
                when(t_pe, 5, npe)
                sc = ps[:, 4, 0:CT * 64].rearrange("p (t j) -> p t j", t=CT)
                step(dve.tensor_reduce(row(6), sc, AX.X, ALU.max))
                step(dve.tensor_tensor(score, sc, wide(row(6)), ALU.subtract), "d_sub")
                when(t_act, 4, na)
                step(dve.tensor_reduce(row(9), score, AX.X, ALU.add))
                step(dve.reciprocal(row(10), row(9)))
                step(dve.tensor_tensor(row(11), row(10), row(5), ALU.mult))
                step(dve.tensor_tensor(prob_bd[0:64, :, 0:64], score[0:64], row(11)[0:64].unsqueeze(2).to_broadcast([64, CT, 64]), ALU.mult))
                step(dve.tensor_tensor(prob_bd[64:128, :, 64:128], score[64:128],
                                       row(11)[64:128].unsqueeze(2).to_broadcast([64, CT, 64]), ALU.mult), "d_p")
                when(t_pe, 7, npe)
                step(dve.tensor_copy(o_t[0:64, :], ps[0:64, 6, :]), "d_o")
                when(t_pe, 8, npe)
                step(dve.tensor_tensor(tok_h2, tok_h, ps[:, 7, 0:CT * 64].rearrange("p (t d) -> p t d", t=CT), ALU.add))
                norm(tok_n2, tok_h2, 6, "d_n2")
                when(t_pe, 10, npe)
                step(dve.tensor_copy(logit, ps[:, 1, 0:CT * E].rearrange("p (t e) -> p t e", t=CT)), alone=True)
                for t in range(CT):
                    step(dve.max(top8[:, t, :], logit[:, t, :]), alone=True)
                    step(dve.max_index(idx_u[:, t, :], top8[:, t, :], logit[:, t, :]), alone=True)
                step(dve.tensor_copy(idx_f, idx_u[:, :, :]))
                step(dve.tensor_tensor(row(7), top8[:, :, 1], top8[:, :, 0], ALU.subtract), "d_dv")
                iota = iota_f.unsqueeze(1).to_broadcast([128, CT, E])
                step(dve.tensor_tensor(oh1, iota, wide(idx_f[:, :, 0], E), ALU.is_equal))
                step(dve.tensor_tensor(oh2, iota, wide(idx_f[:, :, 1], E), ALU.is_equal))
                when(t_act, 8, na)
                step(dve.tensor_scalar(row(9), row(8), 1.0, None, ALU.add))
                step(dve.reciprocal(row(10), row(9)))
                step(dve.tensor_tensor(row(11), row(10), row(8), ALU.mult))
                step(dve.tensor_tensor(oh1, oh1, wide(row(10), E), ALU.mult))
                step(dve.tensor_tensor(oh2, oh2, wide(row(11), E), ALU.mult))
                step(dve.tensor_tensor(gate, oh1, oh2, ALU.add), "d_g")
                when(t_pe, 12, npe)
                step(dve.tensor_tensor(acc, tok_n2, ps[:, 3, 0:CT * 64].rearrange("p (t d) -> p t d", t=CT), ALU.add))
                for e in range(E):
                    dve.wait_ge(t_eo, c * E + e + 1)
                    eo = ps[:, 6 + e % 2, 0:CT * 64].rearrange("p (t d) -> p t d", t=CT)
                    dve.tensor_tensor(weighed, eo, wide(gate[:, :, e]), ALU.mult).then_inc(t_acc, 1)
                    dve.wait_ge(t_acc, c * E + e + 1)
                    step(dve.tensor_tensor(acc, acc, weighed, ALU.add))
                norm(tok_n, acc, 10)
                step(dve.tensor_tensor(tok_c, tok_n, gb_sb[:, 0, :].unsqueeze(1).to_broadcast([128, CT, D]), ALU.mult))
                step(dve.tensor_tensor(tok_q, tok_c, gb_sb[:, 1, :].unsqueeze(1).to_broadcast([128, CT, D]), ALU.add))
                after(dve, st_out, c * 16)
                step(dve.tensor_tensor(tok_o, tok_q, tok_h2, ALU.add))
                assert count[0] == nd
                assert all(TAIL[k] == n for k, n in SEEN.items()), SEEN


TAIL = {"pe": 12, "act": 10, "dve": 77, "d_v1": 6, "d_n1": 8, "d_k": 9, "d_sub": 15, "d_p": 20, "d_o": 21,
        "d_v6": 28, "d_n2": 30, "d_dv": 41, "d_g": 49, "d_v10": 72}
SEEN = {}


def kernel(**inputs):
    import numpy as _np
    import concourse.bacc as _bacc
    from concourse import mybir as _mybir
    from concourse.bass_utils import run_bass_kernel_spmd as _run

    a = {k: _np.asarray(v) for k, v in inputs.items()}
    f = _np.float32
    tok, at, ff = "L0_tok_", "L0_attn_", "L0_ffn_"
    w4 = _np.arange(4)
    x = a["x"].reshape(IMAGES, H, 2, WL * 3).transpose(0, 2, 1, 3).reshape(IMAGES, 128, WL * 3)
    mix = _np.zeros((LAYERS, KHH, MODES, 4, C, 4, C), f)
    conv = _np.zeros((C, 4, LAYERS, C, 4), f)
    for l in range(LAYERS):
        sw = a[f"{tok}sw{l}"].reshape(C, C, KHH, 4, MODES)
        for q in range(4):
            mix[l, :, :, q, :, q, :] = sw[:, :, :, q, :].transpose(2, 3, 0, 1)
            conv[:, q, l, :, q] = a[f"{tok}cw{l}"].T
    mix = mix.reshape(LAYERS * MIXS, MIXN, 128, 128).transpose(0, 2, 1, 3).reshape(LAYERS * MIXS, 128, MIXN * 128)
    convb = _np.stack([a[f"{tok}cb{l}"] for l in range(LAYERS)], 1)
    fc0 = _np.zeros((97, 8, C, 4), f)
    for w in range(WL):
        fc0[3 * w:3 * w + 3, w // 4, :, w % 4] = a[tok + "fc0_w"]
    fc0[96] = a[tok + "fc0_b"][None, :, None]
    fc1 = _np.zeros((C, 4, 2, 2, F1F), f)
    for j in range(2):
        for q in range(2):
            fc1[:, 2 * j + q, j, q, :] = a[tok + "fc1_w"]
    fc1b = _np.concatenate([a[tok + "fc1_b"]] * 2).reshape(128, 1)
    fc2 = _np.zeros((2, F1F, 2), f)
    for q in range(2):
        fc2[q, :, q] = a[tok + "fc2_w"][:, 0]

    def below(w, b):
        return _np.concatenate([w, b.reshape(1, -1)], 0)

    wq, bq, wk, bk = a[at + "Wq"], a[at + "bq"], a[at + "Wk"], a[at + "bk"]
    attn = _np.concatenate([below(wq.T, bq), below(wk.T, bk), below(a[at + "Wv"].T, a[at + "bv"]),
                            below(wq[0:1].T, bq[0:1]), below(wk[0:1].T, bk[0:1]),
                            below(a[at + "Wo"].T, a[at + "bo"])], 1)
    w1 = _np.concatenate([a[ff + "w1"], a[ff + "b1"][:, None, :]], 1).transpose(1, 0, 2)
    w2 = a[ff + "w2"].transpose(1, 0, 2)
    arrays = {
        "x": x, "dft": dft_constants(), "mix_w": mix, "conv_w": conv.reshape(128, LAYERS, 128), "conv_b": convb,
        "fc0_w": fc0.reshape(97, 1024), "fc1_w": fc1.reshape(128, 2, 128), "fc1_b": fc1b, "fc2_w": fc2.reshape(128, 2),
        "fc2_b": a[tok + "fc2_b"].reshape(1, 1), "attn_w": attn, "moe_w1": w1, "moe_w2": w2,
        "gate_w": below(a[ff + "gate_w"], a[ff + "gate_b"]), "moe_b2": a[ff + "b2"],
        "ln_gb": _np.stack([a[ff + "gamma"], a[ff + "beta"]]),
    }
    nc = _bacc.Bacc("TRN2", target_bir_lowering=False, num_devices=1)
    feed, args = {}, []
    for name, v in arrays.items():
        v = _np.ascontiguousarray(v)
        feed[f"in_{name}"] = v
        args.append(nc.dram_tensor(f"in_{name}", v.shape, _mybir.dt.from_np(v.dtype), kind="ExternalInput").ap())
    out = nc.dram_tensor("out_h", (IMAGES, H, W), _mybir.dt.float32, kind="ExternalOutput").ap()
    h_dram = nc.dram_tensor("h_tokens", (IMAGES, H, W), _mybir.dt.float32, kind="Internal").ap()
    vit_tower(nc, *args, out, h_dram)
    r = _run(nc, [feed], core_ids=[0])
    return r.results[0]["out_h"]
```

```python
import numpy as np
import concourse.bass as bass
from concourse import mybir
from contextlib import ExitStack

IMAGES, H, W, C, MODES, LAYERS = 64, 64, 64, 32, 20, 4
GROUPS = 2
GI = IMAGES // GROUPS
WL = W // 2
KH4, KHH = 4, MODES // 4
KHP = 32
SPEC = KHH * MODES * 2
MIXN = 10
MIXS = KHH * MODES // MIXN
MF = MIXN * 2 * GI
F1F = 64
TOK, D, E, F = IMAGES * H, 64, 16, 128
CH = 1024
CT = CH // 128
HALF = 512
EXPERT_STEPS = (CH // HALF) * E
STEPS = {"pe": 13, "act": 13, "dve": 70}
PLACE = {"var1": 5, "n1": 7, "k": 8, "sub": 13, "p0": 17, "p": 18, "o": 19, "h2": 20, "var2": 25,
         "n2_hl": 29, "diff": 39, "g": 58, "var3": 65}
EPS = 1e-5


assert GROUPS <= 2


def dft_constants():
    k, w, h = np.arange(MODES), np.arange(W), np.arange(H)
    ang_w = 2 * np.pi * np.outer(w, k) / W
    ang_h = 2 * np.pi * np.outer(h, k) / H
    cw, sw, chh, shh = np.cos(ang_w), np.sin(ang_w), np.cos(ang_h), np.sin(ang_h)
    fh = np.zeros((2, H, 2, 2, KHP))
    ih = np.zeros((2, 2, KHP, 2, H))
    for a in range(2):
        fh[a, :, a, 0, :MODES], fh[a, :, a, 1, :MODES] = chh, -shh
        ih[a, 0, :MODES, a, :], ih[a, 1, :MODES, a, :] = chh.T, -shh.T
    fw = np.zeros((2, 2, WL, MODES, 2))
    iw = np.zeros((2 * MODES, 2, 2, WL))
    twice = np.where(k == 0, 1.0, 2.0)[:, None]
    for a in range(2):
        c, s = cw[a * WL:(a + 1) * WL], sw[a * WL:(a + 1) * WL]
        fw[a, 0, :, :, 0], fw[a, 1, :, :, 0] = c, s
        fw[a, 0, :, :, 1], fw[a, 1, :, :, 1] = -s, c
        iw[0::2, a, 0], iw[1::2, a, 0] = twice * c.T, -twice * s.T
        iw[0::2, a, 1], iw[1::2, a, 1] = twice * s.T, twice * c.T
    iw3 = np.concatenate([iw.reshape(40, 128)] * 3 + [np.zeros((8, 128))])
    row = np.arange(128)[:, None]
    parts = [fh.reshape(128, 128), ih.reshape(128, 128), iw3, np.eye(128), fw.reshape(128, 40), row // 40 == 2, row // 40 < 2]
    return (np.concatenate(parts, 1) * np.array([0.125] * 384 + [1.0] * 128 + [0.125] * 40 + [1.0] * 2)).astype(np.float32)


def token_tower(nc, x, dft, mix_w, conv_w, conv_b, fc0_w, fc1_w, fc1_b, fc2_w, fc2_b, h_dram):
    f32, f32r = mybir.dt.float32, mybir.dt.float32r
    ALU, ACT, AX = mybir.AluOpType, mybir.ActivationFunctionType, mybir.AxisListType
    ds = bass.ds

    with ExitStack() as ctx:
        def sb(name, shape, dt=f32):
            return ctx.enter_context(nc.sbuf_tensor(name, shape, dt))

        def sem(name):
            return ctx.enter_context(nc.semaphore(name))

        stored_b = sb("stored_b", [128, GI, 1024])
        spec = sb("spec", [128, KHH * MODES, 2, GI])
        mix_slot = [sb(f"mix_slot{u}", [128, MIXN, 128]) for u in range(2)]
        stage_b = [sb(f"stage_b{u}", [128, 8, 128]) for u in range(2)]
        stage_t = sb("stage_t", [128, KHH, 3, 40], f32r)
        pix = sb("pix", [128, 8, C, 4])
        y_sb = sb("y_sb", [128, KHP, C])
        u_sb = sb("u_sb", [128, 8, C, 4])
        tt_sb = sb("tt_sb", [120, MODES, C], f32r)
        inv_w3 = sb("inv_w3", [120, 128], f32r)
        consts = sb("consts", [128, 554])
        fwd_h, inv_h, inv_w = consts[:, 0:128], consts[:, 128:256], consts[0:120, 256:384]
        in_low, in_high = consts[0:120, 552:553], consts[0:120, 553:554]
        ident, fwd_w = consts[:, 384:512], consts[:, 512:552]
        conv_sb = sb("conv_sb", [128, LAYERS, 128])
        convb_raw = sb("convb_raw", [C, LAYERS])
        convb_sb = sb("convb_sb", [C, LAYERS])
        x_in = [sb(f"x_in{u}", [128, 96]) for u in range(2)]
        xt_sb = sb("xt_sb", [97, 128])
        fc0_sb = sb("fc0_sb", [97, 1024])
        fc1_sb = sb("fc1_sb", [128, 2, 128])
        fc1b_sb = sb("fc1b_sb", [128, 1])
        fc2_sb = sb("fc2_sb", [128, 4, 8])
        fc2b_sb = sb("fc2b_sb", [8, 1])
        h_row = sb("h_row", [8, 2, 512])
        b_last = y_sb[:, :, :].rearrange("p a b -> p (a b)")
        g_sb = sb("g_sb", [128, 2, 512])

        ps = ctx.enter_context(nc.psum_tensor("ps", [128, 8, 512], f32))
        x_ps, y_ps, u_ps, t_ps = ps[:, 0:2], ps[:, 2:4], ps[:, 4:6], ps[:, 6:8]
        s_ps = ps[:, 2, 0:SPEC]
        h_ps = ps[0:8, 0, :]

        ld_const = sem("ld_const")
        init_done, inv_w_cut = sem("init_done"), sem("inv_w_cut")
        ld_x = [sem(f"ld_x{u}") for u in range(2)]
        ld_mix = [sem(f"ld_mix{u}") for u in range(2)]
        pe_xt, pe_x, pe_bt, pe_y, pe_s = sem("pe_xt"), sem("pe_x"), sem("pe_bt"), sem("pe_y"), sem("pe_s")
        pe_tt, pe_u, pe_mix, pe_fc1, pe_fc2 = sem("pe_tt"), sem("pe_u"), sem("pe_mix"), sem("pe_fc1"), sem("pe_fc2")
        act_pix, act_b, act_mix, act_g = sem("act_pix"), sem("act_b"), sem("act_mix"), sem("act_g")
        dve_xt, dve_tt, dve_u, dve_y = sem("dve_xt"), sem("dve_tt"), sem("dve_u"), sem("dve_y")
        dve_s, dve_mix, dve_cb, dve_h = sem("dve_s"), sem("dve_mix"), sem("dve_cb"), sem("dve_h")
        pool_b, dve_high, dve_t = sem("pool_b"), sem("dve_high"), sem("dve_t")
        st_h = [sem(f"st_h{u}") for u in range(2)]

        counted = [pe_xt, pe_x, pe_bt, pe_y, pe_s, pe_tt, pe_u, pe_mix, pe_fc1, pe_fc2, act_pix, act_b, act_mix, act_g,
                   dve_xt, dve_tt, dve_u, dve_y, dve_s, dve_mix, dve_cb, dve_h, pool_b, dve_high, dve_t, *st_h]

        passed = sem("passed")

        def after(eng, s, n):
            eng.wait_ge(s, n + 1)

        block = ctx.enter_context(nc.Block())

        def image_loop(eng, body):
            body(0, None, 0, True, False)
            with eng.Fori(0, (GI - 2) // 2) as p:
                for k in range(2):
                    body(p * 2 + (1 + k), p * 2 + k, (1 + k) % 2, False, False)
            body(GI - 1, GI - 2, (GI - 1) % 2, False, True)

        NCONST = 9

        @block.sync
        def _(sp):
            for s in counted:
                sp.sem_inc(s, 1)
            for dst, src in ((consts[:, :], dft), (fc0_sb[:, :], fc0_w), (conv_sb[:, :, :], conv_w),
                             (convb_raw[:, :], conv_b), (fc1_sb[:, :, :], fc1_w), (fc1b_sb[:, :], fc1_b),
                             (fc2_sb[:, :, :], fc2_w), (fc2b_sb[:, :], fc2_b.to_broadcast([8, 1]))):
                sp.dma_start(dst, src).then_inc(ld_const, 16)

            def load_x(g, i, u, free):
                after(sp, pe_xt, free)
                sp.dma_start(x_in[u][:, :], x[ds(g * GI + i, 1)].rearrange("b p f -> p (b f)")).then_inc(ld_x[u], 16)

            def load_mix(s, u, free):
                after(sp, pe_mix, free)
                sp.dma_start(mix_slot[u][:, :, :].rearrange("p m o -> p (m o)"),
                             mix_w[ds(s, 1)].rearrange("s p f -> p (s f)")).then_inc(ld_mix[u], 16)

            with sp.Fori(0, GROUPS) as g:
                load_x(g, 0, 0, g * GI)
                load_x(g, 1, 1, g * GI)
                with sp.Fori(0, GI // 2 - 1) as p:
                    for u in range(2):
                        load_x(g, p * 2 + 2 + u, u, g * GI + p * 2 + u + 1)
                steps = LAYERS * MIXS
                load_mix(0, 0, g * (steps - 1))
                load_mix(1, 1, g * steps)
                with sp.Fori(0, steps // 2 - 1) as p:
                    for u in range(2):
                        load_mix(p * 2 + 2 + u, u, g * steps + p * 2 + 1 + u)
                with sp.Fori(0, GI // 2) as p:
                    for u in range(2):
                        m = g * GI + p * 2 + u
                        after(sp, dve_h, m + 1)
                        sp.dma_start(h_dram[ds(m, 1)].rearrange("m (r c) h -> (m r) (c h)", r=8),
                                     h_row[:, u, :]).then_inc(st_h[u], 16)
            for u in range(2):
                after(sp, st_h[u], 16 * IMAGES // 2)
        @block.gpsimd
        def _(gp):
            gp.memset(xt_sb[:, :], 1.0).then_inc(init_done, 1)
            with gp.Fori(0, GROUPS) as g:
                with gp.Fori(0, LAYERS) as layer:
                    xbase = (g * (LAYERS + 1) + layer + 1) * GI
                    after(gp, act_b, xbase)

                    def stage(i, u, reads):
                        if reads is not None:
                            after(gp, pe_x, reads)
                        gp.sem_inc(passed, 1)
                        gp.tensor_copy(stage_b[u][:, :, :].rearrange("p a b -> p (a b)"),
                                       stored_b[:, ds(i, 1), :].rearrange("p a b -> p (a b)")).then_inc(pool_b, 1)
                    stage(0, 0, None)
                    stage(1, 1, None)
                    with gp.Fori(0, GI // 2 - 1) as p:
                        for u in range(2):
                            stage(p * 2 + 2 + u, u, xbase + p * 2 + u + 1)

        @block.tensor
        def _(pe):
            mm = pe.matmul
            a_flat = pix[:, :, :, :].rearrange("p (a b) c w -> p a (b c w)", a=2)
            pe.wait_ge(ld_const, 16 * (NCONST - 1))
            pe.wait_ge(init_done, 2)
            pe.wait_ge(inv_w_cut, 4)

            def transpose_pixels(n):
                after(pe, act_pix, n + 1)
                for b in range(8):
                    src = pix[:, b, :, :].rearrange("p c w -> p (c w)")
                    last = pe.transpose(t_ps[:, b // 4, (b % 4) * 128:(b % 4 + 1) * 128], src, ident)
                last.then_inc(pe_bt, 1)

            def forward_h(f):
                after(pe, dve_s, f)
                for a in range(2):
                    last = mm(y_ps[:, a, :], fwd_h, a_flat[:, a, :], start=True, stop=True)
                last.then_inc(pe_y, 1)

            def forward_w(f):
                after(pe, dve_y, f + 1)
                y = y_sb[:, :, :].rearrange("p k c -> p (k c)")
                for k in range(KHH):
                    last = mm(s_ps[:, k * 40:(k + 1) * 40], y[:, k * 128:(k + 1) * 128], fwd_w, start=True, stop=True)
                last.then_inc(pe_s, 1)

            def transpose_spec(v, n_before):
                after(pe, dve_t, v + 1)
                after(pe, act_b, n_before)
                pe.sem_inc(passed, 1)
                for k in range(KHH):
                    last = pe.transpose(t_ps[0:120, k // 4, (k % 4) * 128:(k % 4 + 1) * 128],
                                        stage_t[:, k, :, :].rearrange("p a b -> p (a b)").bitcast(f32), ident)
                last.then_inc(pe_tt, 1)

            def inverse_w(v):
                after(pe, dve_tt, v + 1)
                after(pe, dve_u, v)
                t = tt_sb[:, :, :].rearrange("p k o -> p (k o)")
                mm(u_ps[:, 0, :], inv_w3[:, :], t[:, 0:512], start=True, stop=True)
                mm(u_ps[:, 1, 0:128], inv_w3[:, :], t[:, 512:640], start=True, stop=True).then_inc(pe_u, 1)

            def conv_inverse_h(layer, u, v):
                after(pe, pool_b, v + 1)
                after(pe, dve_u, v + 1)
                wc = conv_sb[:, ds(layer, 1), :].rearrange("p a b -> p (a b)")
                uf = u_sb[:, :, :, :].rearrange("p (a b) o w -> p a (b o w)", a=2)
                for a in range(2):
                    mm(x_ps[:, a, :], inv_h, uf[:, a, :], start=True, stop=False, skip_group_check=True)
                    for b in range(4):
                        last = mm(x_ps[:, a, b * 128:(b + 1) * 128], stage_b[u][:, a * 4 + b, :], wc, start=False, stop=(b == 3), skip_group_check=True)
                last.then_inc(pe_x, 1)

            def transpose_x(m, u, lds, n_before):
                pe.wait_ge(ld_x[u], lds)
                after(pe, act_b, n_before)
                pe.transpose(t_ps[0:96, 0, 0:128], x_in[u][:, :], ident).then_inc(pe_xt, 1)

            def lift(m):
                after(pe, dve_xt, m + 1)
                for a in range(2):
                    last = mm(x_ps[:, a, :], xt_sb[:, :], fc0_sb[:, a * 512:(a + 1) * 512], start=True, stop=True)
                last.then_inc(pe_x, 1)

            def mix(g, layer):
                gl = g * LAYERS + layer
                after(pe, dve_s, gl * GI + GI)
                after(pe, act_b, (g * (LAYERS + 1) + layer + 1) * GI)
                pe.sem_inc(passed, 1)
                with pe.Fori(0, MIXS // 2) as p:
                    for u, dst in ((0, (x_ps, y_ps)), (1, (t_ps, u_ps))):
                        done = gl * (MIXS // 2) + p
                        pe.wait_ge(ld_mix[u], done * 16 + 16)
                        after(pe, (dve_mix, act_mix)[u], done)
                        for m in range(MIXN):
                            src = spec[:, ds((p * 2 + u) * MIXN + m, 1), :, :].rearrange("p a r i -> p (a r i)")
                            for k in range(2):
                                o = dst[k][0:64].rearrange("p a b -> p (a b)")[:, m * 2 * GI:(m + 1) * 2 * GI]
                                last = mm(o, mix_slot[u][:, m, k * 64:(k + 1) * 64], src, start=True, stop=True)
                        last.then_inc(pe_mix, 1)
                done = (gl + 1) * (MIXS // 2)
                after(pe, dve_mix, done)
                after(pe, act_mix, done)

            with pe.Fori(0, GROUPS) as g:
                nb = g * (LAYERS + 1) * GI
                transpose_x(g * GI, 0, g * (16 * GI // 2) + 16, nb)

                def first_pass(i, prev, u, first, last):
                    m, n, f = g * GI + i, nb + i, g * LAYERS * GI + i
                    after(pe, act_pix, n)
                    lift(m)
                    if not last:
                        transpose_x(m + 1, 1 - u, g * (16 * GI // 2) + (i + u) * 8 + 16, n)
                    if not first:
                        forward_w(f - 1)
                    if not last:
                        after(pe, dve_xt, m + 2)
                    transpose_pixels(n)
                    forward_h(f)

                image_loop(pe, first_pass)
                forward_w(g * LAYERS * GI + GI - 1)

                with pe.Fori(0, LAYERS - 1) as layer:
                    mix(g, layer)
                    v0, n0, f0 = (g * LAYERS + layer) * GI, nb + (layer + 1) * GI, (g * LAYERS + layer + 1) * GI
                    transpose_spec(v0, n0)
                    inverse_w(v0)

                    def layer_pass(i, prev, u, first, last):
                        v, n, f = v0 + i, n0 + i, f0 + i
                        conv_inverse_h(layer, u, v)
                        if not last:
                            transpose_spec(v + 1, n)
                        if not first:
                            forward_w(f - 1)
                        if not last:
                            inverse_w(v + 1)
                        transpose_pixels(n)
                        forward_h(f)

                    image_loop(pe, layer_pass)
                    forward_w(f0 + GI - 1)

                mix(g, LAYERS - 1)
                v0, n0 = (g * LAYERS + LAYERS - 1) * GI, nb + LAYERS * GI
                transpose_spec(v0, n0)
                inverse_w(v0)

                def fc1(m, c):
                    if c >= 2:
                        after(pe, act_g, m * 4 + c - 1)
                    mm(y_ps[:, c % 2, :], fc1_sb[:, c % 2, :], b_last[:, (c // 2) * 512:(c // 2 + 1) * 512],
                       start=True, stop=True).then_inc(pe_fc1, 1)

                def fc2(m, c):
                    after(pe, act_g, m * 4 + c + 1)
                    mm(h_ps, fc2_sb[:, c, :], g_sb[:, c % 2, :], start=c == 0, stop=c == 3).then_inc(pe_fc2, 1)

                def head(m, n, pixels, between):
                    after(pe, act_b, n + 1)
                    fc1(m, 0)
                    fc1(m, 1)
                    between()
                    after(pe, act_pix, pixels)
                    fc2(m, 0)
                    fc1(m, 2)
                    fc2(m, 1)
                    fc1(m, 3)
                    fc2(m, 2)
                    fc2(m, 3)

                def last_pass(i, prev, u, first, last):
                    v, n = v0 + i, n0 + i
                    after(pe, dve_h, g * GI + (0 if prev is None else prev))
                    conv_inverse_h(LAYERS - 1, u, v)
                    if not last:
                        transpose_spec(v + 1, n)
                    next_w = (lambda: None) if last else (lambda: inverse_w(v + 1))
                    if first:
                        next_w()
                    else:
                        head(g * GI + prev, n0 + prev, n + 1, next_w)
                    transpose_pixels(n)

                image_loop(pe, last_pass)
                after(pe, dve_h, g * GI + GI - 1)
                head(g * GI + GI - 1, n0 + GI - 1, n0 + GI, lambda: None)
                after(pe, dve_h, g * GI + GI)

        @block.scalar
        def _(act):
            pix_f = pix[:, :, :, :].rearrange("p a c w -> p (a c w)")
            x_f = x_ps.rearrange("p a b -> p (a b)")
            t_f = t_ps.rearrange("p a b -> p (a b)")

            def to_pixels(n, func):
                after(act, pe_x, n + 1)
                after(act, pe_bt, n)
                act.activation(pix_f, x_f, func).then_inc(act_pix, 1)

            def store_b(n, dst):
                after(act, pe_bt, n + 1)
                act.activation(dst, t_f, ACT.Copy).then_inc(act_b, 1)

            with act.Fori(0, GROUPS) as g:
                nb = g * (LAYERS + 1) * GI

                def stored(i):
                    return stored_b[:, ds(i, 1), :].rearrange("p a b -> p (a b)")

                def first_pass(i, prev, u, first, last):
                    after(act, pe_y, g * LAYERS * GI + i)
                    to_pixels(nb + i, ACT.Copy)
                    store_b(nb + i, stored(i))

                image_loop(act, first_pass)

                def mix_evac(layer):
                    with act.Fori(0, MIXS // 2) as p:
                        gl = g * LAYERS + layer
                        after(act, pe_mix, gl * MIXS + p * 2 + 2)
                        for k, src in enumerate((t_ps, u_ps)):
                            dst = spec[k * 64:(k + 1) * 64, ds((p * 2 + 1) * MIXN, MIXN), :, :].rearrange("p m r i -> p (m r i)")
                            last = act.activation(dst, src[0:64].rearrange("p a b -> p (a b)")[:, 0:MF], ACT.Copy)
                        last.then_inc(act_mix, 1)

                with act.Fori(0, LAYERS - 1) as layer:
                    mix_evac(layer)

                    def layer_pass(i, prev, u, first, last):
                        after(act, pe_y, (g * LAYERS + layer + 1) * GI + i)
                        to_pixels(nb + (layer + 1) * GI + i, ACT.Gelu)
                        store_b(nb + (layer + 1) * GI + i, stored(i))

                    image_loop(act, layer_pass)
                mix_evac(LAYERS - 1)

                def head(m):
                    for c in range(4):
                        after(act, pe_fc1, m * 4 + c + 1)
                        after(act, pe_fc2, m * 4 + c - 1 if c >= 2 else m * 4)
                        act.activation(g_sb[:, c % 2, :], y_ps[:, c % 2, :], ACT.Gelu, bias=fc1b_sb[:, :]).then_inc(act_g, 1)

                def last_pass(i, prev, u, first, last):
                    n, m = nb + LAYERS * GI + i, g * GI + i
                    to_pixels(n, ACT.Gelu)
                    if not first:
                        head(g * GI + prev)
                    store_b(n, b_last)

                image_loop(act, last_pass)
                head(g * GI + GI - 1)

        @block.vector
        def _(dve):
            dve.memset(u_ps, 0.0).then_inc(init_done, 1)
            dve.wait_ge(ld_const, 16 * (NCONST - 1))
            dve.tensor_scalar(convb_sb[:, :], convb_raw[:, :], float(H * W) ** 0.5, None, ALU.mult).then_inc(dve_cb, 1)
            after(dve, dve_cb, 1)
            dve.wait_ge(init_done, 2)

            rounded = y_sb[0:120, :, :].rearrange("p a b -> p (a b)")[:, 0:128].bitcast(f32r)
            rest, low = u_sb[0:120, 0, 0:32, :], u_sb[0:120, 1, 0:32, :]
            rest, low = rest.rearrange("p a b -> p (a b)"), low.rearrange("p a b -> p (a b)")
            dve.tensor_copy(rounded, inv_w).then_inc(inv_w_cut, 1)
            dve.wait_ge(inv_w_cut, 1)
            dve.tensor_tensor(rest, inv_w, rounded.bitcast(f32), ALU.subtract).then_inc(inv_w_cut, 1)
            dve.wait_ge(inv_w_cut, 2)
            dve.tensor_scalar(low, rest, in_low, None, ALU.mult).then_inc(inv_w_cut, 1)
            dve.wait_ge(inv_w_cut, 3)
            dve.scalar_tensor_tensor(inv_w3[:, :], rounded.bitcast(f32), in_high, low, ALU.mult, ALU.add).then_inc(inv_w_cut, 1)
            dve.wait_ge(inv_w_cut, 4)

            def stage_spec(v, i):
                after(dve, pe_tt, v)
                src = spec[:, :, :, ds(i, 1)].rearrange("p (a k) r c -> p a (k r c)", a=KHH)
                for part in (0, 2):
                    dve.tensor_copy(stage_t[:, :, part, :], src).then_inc(dve_high, 1)
                after(dve, dve_high, 2 * v + 2)
                dve.tensor_tensor(stage_t[:, :, 1, :], src, stage_t[:, :, 0, :].bitcast(f32), ALU.subtract).then_inc(dve_t, 1)

            def copy_tt(v):
                after(dve, pe_tt, v + 1)
                after(dve, pe_u, v)
                dve.tensor_copy(tt_sb[:, :, :].rearrange("p k o -> p (k o)"),
                                t_ps[0:120].rearrange("p a b -> p (a b)")[:, 0:640]).then_inc(dve_tt, 1)

            def turn_u(v, n):
                after(dve, pe_u, v + 1)
                after(dve, pe_x, n)
                src = u_ps.rearrange("p a (k o) -> p o (a k)", o=C)
                dve.transpose(u_sb[:, :, :, :].rearrange("p b o w -> p o b w"), src).then_inc(dve_u, 1)

            def turn_y(f):
                after(dve, pe_y, f + 1)
                after(dve, pe_s, f)
                src = y_ps.rearrange("p a (b c w) -> p c (a b) w", b=4, w=4)
                dve.transpose(y_sb[:, :, :].rearrange("p k c -> p c k"), src).then_inc(dve_y, 1)

            def keep_spec(f, i):
                after(dve, pe_s, f + 1)
                dve.tensor_copy(spec[:, :, :, ds(i, 1)].rearrange("p a b c -> p (a b c)"), s_ps).then_inc(dve_s, 1)

            with dve.Fori(0, GROUPS) as g:
                nb = g * (LAYERS + 1) * GI

                def copy_xt(m, n):
                    after(dve, pe_xt, m + 1)
                    after(dve, pe_x, n)
                    dve.tensor_copy(xt_sb[0:96, :], t_ps[0:96, 0, 0:128]).then_inc(dve_xt, 1)

                copy_xt(g * GI, nb)

                def first_pass(i, prev, u, first, last):
                    m, f = g * GI + i, g * LAYERS * GI + i
                    if not last:
                        copy_xt(m + 1, nb + i + 1)
                    if not first:
                        keep_spec(f - 1, i - 1)
                    turn_y(f)

                image_loop(dve, first_pass)
                keep_spec(g * LAYERS * GI + GI - 1, GI - 1)

                def mix_evac(layer):
                    gl = g * LAYERS + layer
                    with dve.Fori(0, MIXS // 2) as p:
                        after(dve, pe_mix, gl * MIXS + p * 2 + 1)
                        for k, src in enumerate((x_ps, y_ps)):
                            dst = spec[k * 64:(k + 1) * 64, ds((p * 2) * MIXN, MIXN), :, :].rearrange("p m r i -> p (m r i)")
                            last = dve.tensor_copy(dst, src[0:64].rearrange("p a b -> p (a b)")[:, 0:MF])
                        last.then_inc(dve_mix, 1)
                    after(dve, dve_mix, (gl + 1) * (MIXS // 2))
                    mode0 = spec[0:C, 0, 0, :]
                    dve.tensor_tensor(mode0, mode0, convb_sb[:, ds(layer, 1)].to_broadcast([C, GI]), ALU.add).then_inc(dve_cb, 1)
                    after(dve, dve_cb, gl + 2)
                    after(dve, act_mix, (gl + 1) * (MIXS // 2))

                with dve.Fori(0, LAYERS - 1) as layer:
                    mix_evac(layer)
                    v0, n0, f0 = (g * LAYERS + layer) * GI, nb + (layer + 1) * GI, (g * LAYERS + layer + 1) * GI
                    stage_spec(v0, 0)
                    copy_tt(v0)
                    turn_u(v0, n0)

                    def layer_pass(i, prev, u, first, last):
                        if not last:
                            stage_spec(v0 + i + 1, i + 1)
                            copy_tt(v0 + i + 1)
                        if not first:
                            keep_spec(f0 + i - 1, i - 1)
                        if not last:
                            turn_u(v0 + i + 1, n0 + i + 1)
                        turn_y(f0 + i)

                    image_loop(dve, layer_pass)
                    keep_spec(f0 + GI - 1, GI - 1)

                mix_evac(LAYERS - 1)
                v0, n0 = (g * LAYERS + LAYERS - 1) * GI, nb + LAYERS * GI
                stage_spec(v0, 0)
                copy_tt(v0)
                turn_u(v0, n0)

                def keep_h(m, u):
                    after(dve, pe_fc2, (m + 1) * 4)
                    after(dve, st_h[u], (m - u) * 8)
                    dve.tensor_scalar(h_row[:, u, :], h_ps, fc2b_sb[:, :], None, ALU.add).then_inc(dve_h, 1)

                def last_pass(i, prev, u, first, last):
                    if not last:
                        stage_spec(v0 + i + 1, i + 1)
                        copy_tt(v0 + i + 1)
                        turn_u(v0 + i + 1, n0 + i + 1)
                    if not first:
                        keep_h(g * GI + prev, 1 - u)

                image_loop(dve, last_pass)
                keep_h(g * GI + GI - 1, (GI - 1) % 2)


def attention_and_experts(nc, h_dram, attn_w, moe_w1, moe_b1, moe_w2, moe_b2, gate_w, gate_b, selector, eye,
                          column_order, ln_gb, out):
    f32, f32r, u32 = mybir.dt.float32, mybir.dt.float32r, mybir.dt.uint32
    ALU, ACT, AX = mybir.AluOpType, mybir.ActivationFunctionType, mybir.AxisListType
    ds = bass.ds

    with ExitStack() as ctx:
        def sb(name, shape, dt=f32):
            return ctx.enter_context(nc.sbuf_tensor(name, shape, dt))

        def sem(name):
            return ctx.enter_context(nc.semaphore(name))

        h_in = sb("h_in", [D, CH])
        tok_h = sb("tok_h", [128, CT, D])
        centred = sb("centred", [128, CT, D])
        squares = sb("squares", [128, CT, D])
        tok_n = sb("tok_n", [128, CT, D])
        xt = sb("xt", [D + 1, CH])
        q_t = sb("q_t", [D, CH])
        k_t = sb("k_t", [D, CH])
        v_sb = sb("v_sb", [128, CT, D + 2])
        score = sb("score", [128, CT, H])
        prob_bd = sb("prob_bd", [128, CT, 128])
        prob_t = sb("prob_t", [128, CT, 128])
        o_t = sb("o_t", [D + 1, CH])
        tok_h2 = sb("tok_h2", [128, CT, D])
        tok_n2 = sb("tok_n2", [128, CT, D])
        n2_hl = sb("n2_hl", [128, CT, 2, D], f32r)
        x_hl = sb("x_hl", [128, CH], f32r)
        logit = sb("logit", [128, CT, E])
        top8 = sb("top8", [128, CT, 8])
        idx_u = sb("idx_u", [128, CT, 8], u32)
        idx_f = sb("idx_f", [128, CT, 8])
        iota_u = sb("iota_u", [128, E], mybir.dt.int32)
        iota_f = sb("iota_f", [128, E])
        oh1 = sb("oh1", [128, CT, E])
        oh2 = sb("oh2", [128, CT, E])
        gate = sb("gate", [128, CT, E])
        gate_hl = sb("gate_hl", [128, CT, 2, E], f32r)
        gate_t = sb("gate_t", [2 * E, CH], f32r)
        relu = [sb(f"relu{u}", [128, HALF]) for u in range(3)]
        gated = [sb(f"gated{u}", [128, HALF]) for u in range(3)]
        gated_h = [sb(f"gated_h{u}", [128, HALF], f32r) for u in range(3)]
        gated_l = [sb(f"gated_l{u}", [128, HALF], f32r) for u in range(3)]
        z_sb = sb("z_sb", [128, CH])
        acc1 = sb("acc1", [128, CT, D])
        acc2 = sb("acc2", [128, CT, D])
        tok_o = sb("tok_o", [128, CT, D])
        stat = sb("stat", [128, 14, CT])
        attn_sb = sb("attn_sb", [D + 1, 4 * D + 2])
        ident = sb("ident", [128, 128])
        order = sb("order", [D, D])
        gate_sb = sb("gate_sb", [128, E])
        gateb_sb = sb("gateb_sb", [128, E])
        gb_sb = sb("gb_sb", [128, 2, D])
        b1_sb = sb("b1_sb", [128, E])
        w1_raw = sb("w1_raw", [128, E, F])
        w2_raw = sb("w2_raw", [128, E, D])
        b2_raw = sb("b2_raw", [2 * E, D])
        sel_raw = sb("sel_raw", [2 * E, E, 128])
        w1_h = sb("w1_h", [128, E, F], f32r)
        w1_l = sb("w1_l", [128, E, F], f32r)
        w2_hl = sb("w2_hl", [128, E, 2, D], f32r)
        b2_hl = sb("b2_hl", [2 * E, 2, D], f32r)
        sel = sb("sel", [2 * E, E, 128], f32r)

        bank = ctx.enter_context(nc.psum_tensor("bank", [128, 8, 512], f32))

        ld_attn, ld_moe, ld_tok = sem("ld_attn"), sem("ld_moe"), sem("ld_tok")
        st_out = sem("st_out")
        weights_cut, tail_init = sem("weights_cut"), sem("tail_init")
        t_pe, t_act, t_dve = sem("t_pe"), sem("t_act"), sem("t_dve")
        up_done, relu_done, gated_done = sem("up_done"), sem("relu_done"), sem("gated_done")
        high_done, low_done, down_done = sem("high_done"), sem("low_done"), sem("down_done")
        counted = [st_out]
        tail_passed = sem("tail_passed")

        NATTN, NMOE = 4, 7
        moe_loads = ((gate_sb, gate_w), (gateb_sb, gate_b.to_broadcast([128, E])), (b1_sb, moe_b1), (b2_raw, moe_b2),
                     (sel_raw, selector), (w1_raw, moe_w1), (w2_raw, moe_w2))
        block = ctx.enter_context(nc.Block())

        UP_BANK, GATE_BANK = (0, 1, 6), (2, 3, 7)

        def whole(t):
            names = " ".join("abc"[:len(t.shape) - 1])
            return t[tuple([slice(None)] * len(t.shape))].rearrange(f"p {names} -> p ({names})") if len(t.shape) > 2 else t[:, :]

        @block.sync
        def _(sp):
            for s in counted:
                sp.sem_inc(s, 1)
            def load(c):
                sp.dma_start(h_in[:, :].rearrange("w (b h) -> w b h", h=H),
                             h_dram[ds(c * (CH // H), CH // H)].rearrange("b w h -> w b h")).then_inc(ld_tok, 16)

            out_rows = out.rearrange("b h w -> (b h) w").rearrange("(c t p) w -> c p t w", t=CT, p=128)
            load(0)
            for dst, src in ((ident[:, :], eye), (order[:, :], column_order), (attn_sb[:, :], attn_w),
                             (gb_sb[:, :, :], ln_gb.rearrange("(o a) d -> o a d", o=1).to_broadcast([128, 2, D]))):
                sp.dma_start(dst, src).then_inc(ld_attn, 16)
            for dst, src in moe_loads:
                sp.dma_start(whole(dst), src).then_inc(ld_moe, 16)

            def store(c):
                sp.wait_ge(t_dve, STEPS["dve"] * (c + 1))
                sp.dma_start(out_rows[ds(c, 1)].rearrange("c p t w -> p (c t) w"), tok_o[:, :, :]).then_inc(st_out, 16)

            with sp.Fori(0, TOK // CH - 1) as c:
                sp.wait_ge(t_pe, c * STEPS["pe"] + 1)
                load(c + 1)
                store(c)
            store(TOK // CH - 1)
            sp.wait_ge(st_out, 1 + 16 * (TOK // CH))

        @block.gpsimd
        def _(gp):
            gp.iota(iota_u[:, :], pattern=[[1, E]], base=0, channel_multiplier=0).then_inc(tail_init, 1)
            gp.wait_ge(ld_moe, 16 * NMOE)
            gp.tensor_copy(whole(sel), whole(sel_raw)).then_inc(weights_cut, 1)
            gp.tensor_copy(b2_hl[:, 0, :], b2_raw[:, :]).then_inc(weights_cut, 1)
            gp.tensor_copy(whole(w1_h), whole(w1_raw)).then_inc(weights_cut, 1)
            gp.tensor_copy(w2_hl[:, :, 0, :], w2_raw[:, :, :]).then_inc(weights_cut, 1)
            gp.wait_ge(weights_cut, 4)
            gp.tensor_tensor(b2_hl[:, 1, :], b2_raw[:, :], b2_hl[:, 0, :].bitcast(f32), ALU.subtract).then_inc(weights_cut, 1)
            gp.tensor_tensor(whole(w1_l), whole(w1_raw), whole(w1_h).bitcast(f32), ALU.subtract).then_inc(weights_cut, 1)
            gp.tensor_tensor(w2_hl[:, :, 1, :], w2_raw[:, :, :], w2_hl[:, :, 0, :].bitcast(f32),
                             ALU.subtract).then_inc(weights_cut, 1)

        @block.tensor
        def _(pe):
            mm = pe.matmul
            pe.wait_ge(ld_attn, 16 * NATTN)
            pe.wait_ge(tail_init, 4)
            with pe.Fori(0, TOK // CH) as c:
                def when(s, k, total):
                    pe.wait_ge(s, c * total + k)

                nd, na, steps = STEPS["dve"], STEPS["act"], EXPERT_STEPS

                def cols(t):
                    return slice(t % 4 * 128, t % 4 * 128 + 128)

                pe.wait_ge(ld_tok, c * 16 + 16)
                pe.sem_inc(tail_passed, 1)
                for t in range(CT):
                    last = mm(bank[:, 4, t * D:(t + 1) * D], h_in[:, t * 128:(t + 1) * 128], order[:, :],
                              start=True, stop=True, skip_group_check=True)
                last.then_inc(t_pe, 1)
                when(t_dve, PLACE["n1"], nd)
                pe.sem_inc(tail_passed, 1)
                for t in range(CT):
                    last = pe.transpose(bank[0:D, t // 4, cols(t)], tok_n[:, t, :], ident[:, :])
                last.then_inc(t_pe, 1)
                when(t_act, 3, na)
                for j, b in ((0, 2), (1, 4)):
                    for half in range(2):
                        last = mm(bank[0:D, b + half, :], attn_sb[:, j * D:(j + 1) * D], xt[:, half * 512:(half + 1) * 512],
                                  start=True, stop=True)
                    last.then_inc(t_pe, 1)
                for t in range(CT):
                    last = mm(bank[:, 6 + t // 4, t % 4 * 66:(t % 4 + 1) * 66], xt[:, t * 128:(t + 1) * 128],
                              attn_sb[:, 2 * D:3 * D + 2], start=True, stop=True, skip_group_check=True)
                last.then_inc(t_pe, 1)
                when(t_act, 4, na)
                when(t_dve, PLACE["k"], nd)
                pe.sem_inc(tail_passed, 1)
                for t in range(CT):
                    for b in range(2):
                        tk = slice(t * 128 + b * 64, t * 128 + b * 64 + 64)
                        last = mm(bank[b * 64:(b + 1) * 64, 0, t * 64:(t + 1) * 64], q_t[:, tk], k_t[:, tk],
                                  start=True, stop=True, skip_group_check=True)
                last.then_inc(t_pe, 1)
                when(t_dve, PLACE["p"], nd)
                for t in range(CT):
                    last = pe.transpose(bank[:, 2 + t // 4, cols(t)], prob_bd[:, t, :], ident[:, :])
                last.then_inc(t_pe, 1)
                when(t_act, 7, na)
                for t in range(CT):
                    last = mm(bank[0:D, 4 + t // 4, cols(t)], v_sb[:, t, 0:D], prob_t[:, t, :],
                              start=True, stop=True, skip_group_check=True)
                last.then_inc(t_pe, 1)
                when(t_dve, PLACE["o"], nd)
                for t in range(CT):
                    last = mm(bank[:, 6, t * D:(t + 1) * D], o_t[:, t * 128:(t + 1) * 128], attn_sb[:, 3 * D + 2:4 * D + 2],
                              start=True, stop=True, skip_group_check=True)
                last.then_inc(t_pe, 1)
                when(t_dve, PLACE["n2_hl"], nd)
                for t in range(CT):
                    last = pe.transpose(bank[:, t // 4, cols(t)],
                                        n2_hl[:, t, :, :].rearrange("p a d -> p (a d)").bitcast(f32), ident[:, :])
                last.then_inc(t_pe, 1)
                pe.wait_ge(ld_moe, 16 * NMOE)
                when(t_act, 9, na)
                for t in range(CT):
                    last = mm(bank[:, 2, t * E:(t + 1) * E], x_hl[:, t * 128:(t + 1) * 128].bitcast(f32), gate_sb[:, :],
                              start=True, stop=True, skip_group_check=True)
                last.then_inc(t_pe, 1)
                when(t_dve, PLACE["g"], nd)
                for t in range(CT):
                    last = pe.transpose(bank[0:2 * E, 4 + t // 4, cols(t)],
                                        gate_hl[:, t, :, :].rearrange("p a e -> p (a e)").bitcast(f32), ident[:, :])
                last.then_inc(t_pe, 1)
                pe.wait_ge(weights_cut, 7)

                def up(k):
                    half, e = k // E, k % E
                    toks = slice(half * HALF, (half + 1) * HALF)
                    if k >= 3:
                        pe.wait_ge(relu_done, c * steps + k - 2)
                    mm(bank[:, UP_BANK[k % 3], :], w1_h[:, e, :], x_hl[:, toks], start=True, stop=False)
                    mm(bank[:, UP_BANK[k % 3], :], w1_l[:, e, :], x_hl[:, toks], start=False, stop=True)
                    if k == 0:
                        when(t_act, 11, na)
                    if k >= 3:
                        pe.wait_ge(gated_done, c * steps + k - 2)
                    mm(bank[:, GATE_BANK[k % 3], :], sel[:, e, :], gate_t[:, toks], start=True, stop=True).then_inc(up_done, 1)

                def down(k):
                    half, e = k // E, k % E
                    z = bank[:, 4 + half, :]
                    if e == 0:
                        mm(z, b2_hl[:, :, :].rearrange("p a d -> p (a d)"), gate_t[:, half * HALF:(half + 1) * HALF],
                           start=True, stop=False)
                    w2 = w2_hl[:, e, :, :].rearrange("p a d -> p (a d)")
                    pe.wait_ge(high_done, c * steps + k + 1)
                    mm(z, w2, gated_h[k % 3][:, :], start=False, stop=False)
                    pe.wait_ge(low_done, c * steps + k + 1)
                    mm(z, w2, gated_l[k % 3][:, :], start=False, stop=e == E - 1).then_inc(down_done, 1)

                up(0)
                up(1)
                up(2)
                for k in range(steps):
                    if k + 3 < steps:
                        up(k + 3)
                    down(k)
                when(t_act, 12, na)
                for t in range(CT):
                    last = pe.transpose(bank[:, t // 4, cols(t)], z_sb[:, t * 128:(t + 1) * 128], ident[:, :])
                last.then_inc(t_pe, 1)

        @block.scalar
        def _(act):
            act.wait_ge(ld_moe, 16 * NMOE)
            with act.Fori(0, TOK // CH) as c:
                def when(s, k, total):
                    act.wait_ge(s, c * total + k)

                npe, nd, steps = STEPS["pe"], STEPS["dve"], EXPERT_STEPS

                def two(b, parts):
                    return bank[0:parts, b:b + 2, :].rearrange("p b f -> p (b f)")

                def root(name):
                    when(t_dve, PLACE[name], nd)
                    act.activation(stat[:, 4, :], stat[:, 3, :], ACT.Sqrt).then_inc(t_act, 1)

                when(t_pe, 1, npe)
                act.activation(whole(tok_h), bank[:, 4, :], ACT.Copy).then_inc(t_act, 1)
                root("var1")
                when(t_pe, 2, npe)
                act.activation(xt[0:D, :], two(0, D), ACT.Copy).then_inc(t_act, 1)
                when(t_pe, 3, npe)
                act.activation(q_t[:, :], two(2, D), ACT.Copy).then_inc(t_act, 1)
                when(t_pe, 5, npe)
                act.activation(v_sb[:, :, :].rearrange("p (b t) d -> p b (t d)", b=2), bank[:, 6:8, 0:4 * 66],
                               ACT.Copy).then_inc(t_act, 1)
                when(t_dve, PLACE["sub"], nd)
                act.activation(whole(score), whole(score), ACT.Exp, scale=float(D) ** -0.5).then_inc(t_act, 1)
                when(t_pe, 7, npe)
                act.activation(whole(prob_t), two(2, 128), ACT.Copy).then_inc(t_act, 1)
                root("var2")
                when(t_pe, 10, npe)
                act.activation(x_hl[:, :], two(0, 128), ACT.Copy).then_inc(t_act, 1)
                when(t_dve, PLACE["diff"], nd)
                act.activation(stat[:, 8, :], stat[:, 7, :], ACT.Exp).then_inc(t_act, 1)
                when(t_pe, 12, npe)
                act.activation(gate_t[:, :], two(4, 2 * E), ACT.Copy).then_inc(t_act, 1)

                def rectify(k):
                    act.wait_ge(up_done, c * steps + k + 1)
                    if k >= 3:
                        act.wait_ge(gated_done, c * steps + k - 2)
                    act.activation(relu[k % 3][:, :], bank[:, UP_BANK[k % 3], :], ACT.Relu,
                                   bias=b1_sb[:, k % E:k % E + 1]).then_inc(relu_done, 1)

                def high(k):
                    act.wait_ge(gated_done, c * steps + k + 1)
                    if k >= 3:
                        act.wait_ge(down_done, c * steps + k - 2)
                    act.activation(gated_h[k % 3][:, :], gated[k % 3][:, :], ACT.Copy).then_inc(high_done, 1)

                rectify(0)
                rectify(1)
                for k in range(steps):
                    if k + 2 < steps:
                        rectify(k + 2)
                    high(k)
                act.wait_ge(down_done, c * steps + steps)
                act.activation(z_sb[:, :], two(4, 128), ACT.Copy).then_inc(t_act, 1)
                root("var3")

        @block.vector
        def _(dve):
            dve.memset(prob_bd[:, :, :], 0.0).then_inc(tail_init, 1)
            dve.memset(xt[D:D + 1, :], 1.0).then_inc(tail_init, 1)
            dve.memset(o_t[D:D + 1, :], 1.0).then_inc(tail_init, 1)
            dve.wait_ge(tail_init, 4)
            dve.tensor_copy(iota_f[:, :], iota_u[:, :]).then_inc(tail_init, 1)
            dve.wait_ge(tail_init, 5)
            dve.wait_ge(ld_attn, 16 * NATTN)
            with dve.Fori(0, TOK // CH) as c:
                nd, npe, na, steps = STEPS["dve"], STEPS["pe"], STEPS["act"], EXPERT_STEPS
                count = [0]

                def step(ins, name=None, alone=False, settle=True):
                    count[0] += 1
                    ins.then_inc(t_dve, 1)
                    if name:
                        assert PLACE[name] == count[0], (name, count[0])
                    if settle:
                        dve.wait_ge(t_dve, c * nd + count[0])
                    if alone:
                        dve.sem_inc(tail_passed, 1)

                def when(s, k, total):
                    dve.wait_ge(s, c * total + k)

                def row(k):
                    return stat[:, k, :]

                def wide(v, n=D):
                    return v.unsqueeze(2).to_broadcast([128, CT, n])

                def norm(dst, src, k, name=None):
                    step(dve.tensor_reduce(row(0), src, AX.X, ALU.add))
                    step(dve.scalar_tensor_tensor(centred[:, :, :], wide(row(0)), -1.0 / D, src, ALU.mult, ALU.add))
                    step(dve.tensor_tensor(squares[:, :, :], centred[:, :, :], centred[:, :, :], ALU.mult))
                    step(dve.tensor_reduce(row(2), squares[:, :, :], AX.X, ALU.add))
                    step(dve.tensor_scalar(row(3), row(2), 1.0 / D, EPS, ALU.mult, ALU.add), f"var{k}")
                    when(t_act, (2, 8, 13)[k - 1], na)
                    step(dve.reciprocal(row(12), row(4)))
                    step(dve.tensor_tensor(dst, centred[:, :, :], wide(row(12)), ALU.mult), name)

                when(t_act, 1, na)
                norm(tok_n[:, :, :], tok_h[:, :, :], 1, "n1")
                when(t_pe, 4, npe)
                step(dve.tensor_copy(k_t[:, :], bank[0:D, 4:6, :].rearrange("p b f -> p (b f)")), "k")
                when(t_act, 5, na)
                step(dve.tensor_scalar(row(5), v_sb[:, :, D], 0.0, None, ALU.not_equal), settle=False)
                step(dve.tensor_scalar(row(6), v_sb[:, :, D + 1], 0.0, None, ALU.not_equal))
                step(dve.tensor_tensor(row(13), row(5), row(6), ALU.mult))
                when(t_pe, 6, npe)
                sc = bank[:, 0, :].rearrange("p (t j) -> p t j", t=CT)
                step(dve.tensor_reduce(row(6), sc, AX.X, ALU.max))
                step(dve.tensor_tensor(score[:, :, :], sc, wide(row(6), H), ALU.subtract), "sub")
                when(t_act, 6, na)
                step(dve.tensor_reduce(row(9), score[:, :, :], AX.X, ALU.add))
                step(dve.reciprocal(row(10), row(9)))
                step(dve.tensor_tensor(row(11), row(10), row(13), ALU.mult))
                for b in range(2):
                    half = slice(b * 64, (b + 1) * 64)
                    step(dve.tensor_tensor(prob_bd[half, :, half], score[half],
                                           row(11)[half].unsqueeze(2).to_broadcast([64, CT, 64]), ALU.mult), ("p0", "p")[b])
                when(t_pe, 8, npe)
                step(dve.tensor_copy(o_t[0:D, :], bank[0:D, 4:6, :].rearrange("p b f -> p (b f)")), "o")
                when(t_pe, 9, npe)
                step(dve.tensor_tensor(tok_h2[:, :, :], tok_h[:, :, :], bank[:, 6, :].rearrange("p (t d) -> p t d", t=CT),
                                       ALU.add), "h2")
                norm(tok_n2[:, :, :], tok_h2[:, :, :], 2)
                step(dve.tensor_copy(n2_hl[:, :, 0, :], tok_n2[:, :, :]))
                step(dve.tensor_tensor(n2_hl[:, :, 1, :], tok_n2[:, :, :], n2_hl[:, :, 0, :].bitcast(f32), ALU.subtract), "n2_hl")
                when(t_pe, 11, npe)
                step(dve.tensor_tensor(logit[:, :, :], bank[:, 2, 0:CT * E].rearrange("p (t e) -> p t e", t=CT),
                                       gateb_sb[:, :].unsqueeze(1).to_broadcast([128, CT, E]), ALU.add), alone=True)
                for t in range(CT):
                    step(dve.max(top8[:, t, :], logit[:, t, :]), settle=t == CT - 1, alone=t == CT - 1)
                step(dve.tensor_tensor(row(7), top8[:, :, 1], top8[:, :, 0], ALU.subtract), "diff", alone=True)
                for t in range(CT):
                    step(dve.max_index(idx_u[:, t, :], top8[:, t, :], logit[:, t, :]), settle=t == CT - 1)
                step(dve.tensor_copy(idx_f[:, :, :], idx_u[:, :, :]))
                iota = iota_f[:, :].unsqueeze(1).to_broadcast([128, CT, E])
                step(dve.tensor_tensor(oh1[:, :, :], iota, wide(idx_f[:, :, 0], E), ALU.is_equal), settle=False)
                step(dve.tensor_tensor(oh2[:, :, :], iota, wide(idx_f[:, :, 1], E), ALU.is_equal), settle=False)
                when(t_act, 10, na)
                step(dve.tensor_scalar(row(9), row(8), 1.0, None, ALU.add))
                step(dve.reciprocal(row(10), row(9)))
                step(dve.tensor_tensor(row(11), row(10), row(8), ALU.mult))
                step(dve.tensor_tensor(oh1[:, :, :], oh1[:, :, :], wide(row(10), E), ALU.mult))
                step(dve.tensor_tensor(oh2[:, :, :], oh2[:, :, :], wide(row(11), E), ALU.mult))
                step(dve.tensor_tensor(gate[:, :, :], oh1[:, :, :], oh2[:, :, :], ALU.add))
                step(dve.tensor_copy(gate_hl[:, :, 0, :], gate[:, :, :]))
                step(dve.tensor_tensor(gate_hl[:, :, 1, :], gate[:, :, :], gate_hl[:, :, 0, :].bitcast(f32), ALU.subtract), "g")

                def weigh(k):
                    dve.wait_ge(relu_done, c * steps + k + 1)
                    if k >= 3:
                        dve.wait_ge(high_done, c * steps + k - 2)
                        dve.wait_ge(low_done, c * steps + k - 2)
                    dve.tensor_tensor(gated[k % 3][:, :], relu[k % 3][:, :], bank[:, GATE_BANK[k % 3], :],
                                      ALU.mult).then_inc(gated_done, 1)

                def low(k):
                    dve.wait_ge(high_done, c * steps + k + 1)
                    if k >= 3:
                        dve.wait_ge(down_done, c * steps + k - 2)
                    dve.tensor_tensor(gated_l[k % 3][:, :], gated[k % 3][:, :], gated_h[k % 3][:, :].bitcast(f32),
                                      ALU.subtract).then_inc(low_done, 1)

                weigh(0)
                for k in range(1, steps):
                    weigh(k)
                    low(k - 1)
                low(steps - 1)
                when(t_pe, 13, npe)
                z = bank[:, 0:2, :].rearrange("p b (t a d) -> p (b t) a d", t=4, a=2)
                step(dve.tensor_tensor(acc1[:, :, :], tok_n2[:, :, :], z[:, :, 0, :], ALU.add))
                step(dve.tensor_tensor(acc2[:, :, :], acc1[:, :, :], z[:, :, 1, :], ALU.add))
                norm(acc1[:, :, :], acc2[:, :, :], 3)
                step(dve.tensor_tensor(acc2[:, :, :], acc1[:, :, :], gb_sb[:, 0, :].unsqueeze(1).to_broadcast([128, CT, D]), ALU.mult))
                step(dve.tensor_tensor(acc1[:, :, :], acc2[:, :, :], gb_sb[:, 1, :].unsqueeze(1).to_broadcast([128, CT, D]), ALU.add))
                dve.wait_ge(st_out, c * 16 + 1)
                step(dve.tensor_tensor(tok_o[:, :, :], acc1[:, :, :], tok_h2[:, :, :], ALU.add))
                assert count[0] == nd, count[0]


def kernel(**inputs):
    import numpy as _np
    import concourse.bacc as _bacc
    from concourse import mybir as _mybir
    from concourse.bass_utils import run_bass_kernel_spmd as _run

    a = {k: _np.asarray(v) for k, v in inputs.items()}
    f = _np.float32
    tok, at, ff = "L0_tok_", "L0_attn_", "L0_ffn_"
    w4 = _np.arange(4)
    x = a["x"].reshape(IMAGES, H, 2, WL * 3).transpose(0, 2, 1, 3).reshape(IMAGES, 128, WL * 3)
    mix = _np.zeros((LAYERS, KHH, MODES, 4, C, 4, C), f)
    conv = _np.zeros((C, 4, LAYERS, C, 4), f)
    for l in range(LAYERS):
        sw = a[f"{tok}sw{l}"].reshape(C, C, KHH, 4, MODES)
        for q in range(4):
            mix[l, :, :, q, :, q, :] = sw[:, :, :, q, :].transpose(2, 3, 0, 1)
            conv[:, q, l, :, q] = a[f"{tok}cw{l}"].T
    mix = mix.reshape(LAYERS * MIXS, MIXN, 128, 128).transpose(0, 2, 1, 3).reshape(LAYERS * MIXS, 128, MIXN * 128)
    convb = _np.stack([a[f"{tok}cb{l}"] for l in range(LAYERS)], 1)
    fc0 = _np.zeros((97, 8, C, 4), f)
    for w in range(WL):
        fc0[3 * w:3 * w + 3, w // 4, :, w % 4] = a[tok + "fc0_w"]
    fc0[96] = a[tok + "fc0_b"][None, :, None]
    fc1 = _np.zeros((C, 4, 2, 2, F1F), f)
    for j in range(2):
        for q in range(2):
            fc1[:, 2 * j + q, j, q, :] = a[tok + "fc1_w"]
    fc1b = _np.concatenate([a[tok + "fc1_b"]] * 2).reshape(128, 1)
    fc2 = _np.zeros((2, F1F, 4, 4, 2), f)
    for q in range(2):
        for c in range(4):
            fc2[q, :, c, c, q] = a[tok + "fc2_w"][:, 0]

    def below(w, b):
        return _np.concatenate([w, b.reshape(1, -1)], 0)

    wq, bq, wk, bk = a[at + "Wq"], a[at + "bq"], a[at + "Wk"], a[at + "bk"]
    attn = _np.concatenate([below(wq.T, bq), below(wk.T, bk), below(a[at + "Wv"].T, a[at + "bv"]),
                            below(wq[0:1].T, bq[0:1]), below(wk[0:1].T, bk[0:1]),
                            below(a[at + "Wo"].T, a[at + "bo"])], 1)
    w1 = a[ff + "w1"].transpose(1, 0, 2).reshape(D, E * F)
    w2 = a[ff + "w2"].transpose(1, 0, 2).reshape(F, E * D)
    sel = _np.tile(_np.eye(E, dtype=f), (2, 1))[:, :, None].repeat(128, 2).reshape(2 * E, E * 128)
    arrays = {
        "x": x, "dft": dft_constants(), "mix_w": mix, "conv_w": conv.reshape(128, LAYERS, 128), "conv_b": convb,
        "fc0_w": fc0.reshape(97, 1024), "fc1_w": fc1.reshape(128, 2, 128), "fc1_b": fc1b, "fc2_w": fc2.reshape(128, 4, 8),
        "fc2_b": a[tok + "fc2_b"].reshape(1, 1), "attn_w": attn,
        "moe_w1": _np.concatenate([w1, w1]), "moe_b1": a[ff + "b1"].T, "moe_w2": w2,
        "moe_b2": _np.concatenate([a[ff + "b2"]] * 2), "gate_w": _np.concatenate([a[ff + "gate_w"]] * 2),
        "gate_b": a[ff + "gate_b"].reshape(1, E), "selector": sel, "eye": _np.eye(128, dtype=f),
        "column_order": _np.eye(D, dtype=f).reshape(2, 2, 4, 4, D).transpose(1, 3, 2, 0, 4).reshape(D, D),
        "ln_gb": _np.stack([a[ff + "gamma"], a[ff + "beta"]]),
    }
    nc = _bacc.Bacc("TRN2", target_bir_lowering=False, num_devices=1)
    feed, args = {}, []
    for name, v in arrays.items():
        v = _np.ascontiguousarray(v)
        feed[f"in_{name}"] = v
        args.append(nc.dram_tensor(f"in_{name}", v.shape, _mybir.dt.from_np(v.dtype), kind="ExternalInput").ap())
    out = nc.dram_tensor("out_h", (IMAGES, H, W), _mybir.dt.float32, kind="ExternalOutput").ap()
    h_dram = nc.dram_tensor("h_tokens", (IMAGES, H, W), _mybir.dt.float32, kind="Internal").ap()
    token_tower(nc, *args[:10], h_dram)
    attention_and_experts(nc, h_dram, *args[10:], out)
    r = _run(nc, [feed], core_ids=[0])
    return r.results[0]["out_h"]
```

```python
import numpy as np
import concourse.bass as bass
from concourse import mybir
from contextlib import ExitStack

IMAGES, H, W, C, MODES, LAYERS = 64, 64, 64, 32, 20, 4
GROUPS = 2
GI = IMAGES // GROUPS
UNROLL = 6
Q = 4
QUADS = GI // Q
WL = W // 2
KHH = MODES // 4
KHP = 32
SPEC = KHH * MODES * 2
MIXN = 10
MIXS = KHH * MODES // MIXN
MF = MIXN * 2 * GI
F1F = 64
TOK, D, E, F = IMAGES * H, 64, 16, 128
CH = 1024
CT = CH // 128
HALF = 512
EXPERT_STEPS = (CH // HALF) * E
STEPS = {"pe": 13, "act": 13, "dve": 62}
PLACE = {"var1": 5, "n1": 7, "k": 8, "sub": 13, "p0": 17, "p": 18, "o": 19, "h2": 20, "var2": 25, "n2_hl": 29,
         "diff": 35, "g": 50, "var3": 57}
EPS = 1e-5

assert GROUPS <= 2
assert (GI - 2) % UNROLL == 0 and UNROLL % 2 == 0


def dft_constants():
    k, w, h = np.arange(MODES), np.arange(W), np.arange(H)
    ang_w = 2 * np.pi * np.outer(w, k) / W
    ang_h = 2 * np.pi * np.outer(h, k) / H
    cw, sw, chh, shh = np.cos(ang_w), np.sin(ang_w), np.cos(ang_h), np.sin(ang_h)
    fh = np.zeros((2, H, 2, 2, KHP))
    ih = np.zeros((2, 2, KHP, 2, H))
    for a in range(2):
        fh[a, :, a, 0, :MODES], fh[a, :, a, 1, :MODES] = chh, -shh
        ih[a, 0, :MODES, a, :], ih[a, 1, :MODES, a, :] = chh.T, -shh.T
    fw = np.zeros((2, 2, WL, MODES, 2))
    iw = np.zeros((2 * MODES, 2, 2, WL))
    twice = np.where(k == 0, 1.0, 2.0)[:, None]
    for a in range(2):
        c, s = cw[a * WL:(a + 1) * WL], sw[a * WL:(a + 1) * WL]
        fw[a, 0, :, :, 0], fw[a, 1, :, :, 0] = c, s
        fw[a, 0, :, :, 1], fw[a, 1, :, :, 1] = -s, c
        iw[0::2, a, 0], iw[1::2, a, 0] = twice * c.T, -twice * s.T
        iw[0::2, a, 1], iw[1::2, a, 1] = twice * s.T, twice * c.T
    iw3 = np.concatenate([iw.reshape(40, 128)] * 3 + [np.zeros((8, 128))])
    row = np.arange(128)[:, None]
    parts = [fh.reshape(128, 128), ih.reshape(128, 128), iw3, np.eye(128), fw.reshape(128, 40), row // 40 == 2, row // 40 < 2]
    return (np.concatenate(parts, 1) * np.array([0.125] * 384 + [1.0] * 128 + [0.125] * 40 + [1.0] * 2)).astype(np.float32)


def token_tower(nc, x_rows, x_cols, dft, mix_w, conv_w, conv_b, fc0_w, fc0_spec, fc1_w, fc1_b, fc2_w, fc2_b, h_dram):
    f32, f32r = mybir.dt.float32, mybir.dt.float32r
    ALU, ACT, AX = mybir.AluOpType, mybir.ActivationFunctionType, mybir.AxisListType
    ds = bass.ds

    with ExitStack() as ctx:
        def sb(name, shape, dt=f32):
            return ctx.enter_context(nc.sbuf_tensor(name, shape, dt))

        def sem(name):
            return ctx.enter_context(nc.semaphore(name))

        stored_b = sb("stored_b", [128, GI, 1024])
        spec = sb("spec", [128, KHH * MODES, 2, GI])
        mix_in = [sb(f"mix_in{u}", [128, MIXN, C]) for u in range(2)]
        mix_slot = [sb(f"mix_slot{u}", [128, MIXN, 128]) for u in range(2)]
        b_cur = sb("b_cur", [128, 1024])
        conv_cur = sb("conv_cur", [128, 128])
        stage_t = sb("stage_t", [128, KHH, 3, 40], f32r)
        pix_h = sb("pix_h", [128, 1024], f32r)
        pix_l = sb("pix_l", [128, 1024], f32r)
        fwd_hh = sb("fwd_hh", [128, 128], f32r)
        fwd_hl = sb("fwd_hl", [128, 128], f32r)
        y_sb = sb("y_sb", [128, KHP, C])
        u_sb = sb("u_sb", [128, 8, C, 4])
        tt_sb = sb("tt_sb", [120, MODES, C], f32r)
        inv_w3 = sb("inv_w3", [120, 128], f32r)
        consts = sb("consts", [128, 554])
        fwd_h, inv_h, inv_w = consts[:, 0:128], consts[:, 128:256], consts[0:120, 256:384]
        in_low, in_high = consts[0:120, 552:553], consts[0:120, 553:554]
        ident, fwd_w = consts[:, 384:512], consts[:, 512:552]
        conv_sb = sb("conv_sb", [128, LAYERS, 128])
        convb_raw = sb("convb_raw", [C, LAYERS])
        convb_sb = sb("convb_sb", [C, LAYERS])
        fc1_sb = sb("fc1_sb", [128, 2, 128])
        fc1b_sb = sb("fc1b_sb", [128, 1])
        fc2_sb = sb("fc2_sb", [128, 4, 8])
        fc2b_sb = sb("fc2b_sb", [8, 1])
        h_row = sb("h_row", [128, 2, 512])
        table = sb("table", [128, 1])
        fc1_h = sb("fc1_h", [128, 2, 128], f32r)
        fc1_l = sb("fc1_l", [128, 2, 128], f32r)
        g_sb = sb("g_sb", [128, 2, 512])
        stage_f = [b_cur, h_row[:, :, :].rearrange("p a b -> p (a b)")]
        x_a = [s[:, 0:Q * 96] for s in stage_f]
        x_b = [s[0:97, 512:1024] for s in stage_f]
        fc0_sb = g_sb[0:97, :, :].rearrange("p a b -> p (a b)")
        lift_sb = u_sb[0:97, 0:5, :, :].rearrange("p a b c -> p (a b c)")
        y_f = y_sb[:, :, :].rearrange("p a b -> p (a b)")
        yx_sb = y_f[:, 0:KHP * 3 * Q]
        sx_sb = y_f[0:97, 512:512 + Q * 40]

        ps = ctx.enter_context(nc.psum_tensor("ps", [128, 8, 512], f32))
        x_ps, y_ps, u_ps, t_ps = ps[:, 0:2], ps[:, 2:4], ps[:, 4:6], ps[:, 6:8]
        s_ps = ps[:, 2, 0:SPEC]
        yx_ps, sx_ps = ps[:, 2, 0:Q * 96], ps[0:3 * MODES, 3, 0:Q * 40]
        h_ps = ps[0:8, 7, :]

        ld_const = sem("ld_const")
        ld_lift = sem("ld_lift")
        ld_x = [sem(f"ld_x{u}") for u in range(2)]
        ld_mix = [sem(f"ld_mix{u}") for u in range(2)]
        st_h = [sem(f"st_h{u}") for u in range(2)]
        init_done, weights_split = sem("init_done"), sem("weights_split")
        pe_yx, pe_sx, pe_lift, pe_b0 = sem("pe_yx"), sem("pe_sx"), sem("pe_lift"), sem("pe_b0")
        dve_yx, dve_sx, dve_lift, dve_bias, act_b0 = sem("dve_yx"), sem("dve_sx"), sem("dve_lift"), sem("dve_bias"), sem("act_b0")
        dve_spread, pool_spread, pool_w = sem("dve_spread"), sem("pool_spread"), sem("pool_w")
        pe_mix, dve_mix, act_mix, dve_cb = sem("pe_mix"), sem("dve_mix"), sem("act_mix"), sem("dve_cb")
        dve_high, dve_t, pe_tt, dve_tt = sem("dve_high"), sem("dve_t"), sem("pe_tt"), sem("dve_tt")
        pe_u, dve_u, pe_x = sem("pe_u"), sem("dve_u"), sem("pe_x")
        act_b, act_hi, dve_lo = sem("act_b"), sem("act_hi"), sem("dve_lo")
        pool_b, pe_bt, pe_y, dve_y = sem("pool_b"), sem("pe_bt"), sem("pe_y"), sem("dve_y")
        pe_s, dve_s = sem("pe_s"), sem("dve_s")
        pe_fc1, act_g, pe_fc2, dve_h = sem("pe_fc1"), sem("act_g"), sem("pe_fc2"), sem("dve_h")

        counted = [pe_yx, pe_sx, pe_lift, pe_b0, dve_yx, dve_sx, dve_lift, act_b0,
                   dve_spread, pool_spread, pool_w, pe_mix, dve_mix, act_mix, dve_cb,
                   dve_high, dve_t, pe_tt, dve_tt, pe_u, dve_u, pe_x, act_b, act_hi, dve_lo,
                   pool_b, pe_bt, pe_y, dve_y, pe_s, dve_s, pe_fc1, act_g, pe_fc2, dve_h, *st_h]

        passed = sem("passed")

        def after(eng, s, n):
            eng.wait_ge(s, n + 1)

        block = ctx.enter_context(nc.Block())

        def image_loop(eng, body):
            body(0, None, 0, True, False)
            with eng.Fori(0, (GI - 2) // UNROLL) as p:
                for k in range(UNROLL):
                    body(p * UNROLL + (1 + k), p * UNROLL + k, (1 + k) % 2, False, False)
            body(GI - 1, GI - 2, (GI - 1) % 2, False, True)

        NCONST = 7

        def spread(eng, blocks, done, gl, p, u):
            eng.wait_ge(ld_mix[u], (gl * (MIXS // 2) + p) * 16 + 16)
            after(eng, pe_mix, gl * MIXS + p * 2 if isinstance(p, int) and p == 0 else gl * MIXS + p * 2 + u - 1)
            eng.sem_inc(passed, 1)
            for q in blocks:
                rows = slice(q * C, (q + 1) * C)
                last = eng.tensor_copy(mix_slot[u][rows, :, rows], mix_in[u][rows, :, :])
            last.then_inc(done, 1)

        @block.sync
        def _(sp):
            for s in counted:
                sp.sem_inc(s, 1)
            for dst, src in ((consts[:, :], dft), (conv_sb[:, :, :], conv_w),
                             (convb_raw[:, :], conv_b), (fc1_sb[:, :, :], fc1_w), (fc1b_sb[:, :], fc1_b),
                             (fc2_sb[:, :, :], fc2_w), (fc2b_sb[:, :], fc2_b.to_broadcast([8, 1]))):
                sp.dma_start(dst, src).then_inc(ld_const, 16)

            def load_x(q, u, free):
                after(sp, pe_lift, free)
                sp.dma_start(x_a[u], x_rows[ds(q, 1)].rearrange("q p f -> p (q f)")).then_inc(ld_x[u], 16)
                sp.dma_start(x_b[u], x_cols[ds(q, 1)].rearrange("q p f -> p (q f)")).then_inc(ld_x[u], 16)

            def load_mix(s, u, free):
                after(sp, dve_spread, free)
                after(sp, pool_spread, free)
                sp.dma_start(mix_in[u][:, :, :].rearrange("p m o -> p (m o)"),
                             mix_w[ds(s, 1)].rearrange("s p f -> p (s f)")).then_inc(ld_mix[u], 16)

            with sp.Fori(0, GROUPS) as g:
                after(sp, pe_x, g * LAYERS * GI)
                after(sp, pe_fc2, g * GI * 4)
                for u in range(2):
                    after(sp, st_h[u], g * 8 * GI)
                sp.sem_inc(passed, 1)
                q0 = g * QUADS
                load_x(q0, 0, q0)
                sp.dma_start(fc0_sb, fc0_w).then_inc(ld_lift, 16)
                sp.dma_start(lift_sb, fc0_spec).then_inc(ld_lift, 16)
                load_x(q0 + 1, 1, q0)
                steps = LAYERS * MIXS
                load_mix(0, 0, g * (steps - 1))
                load_mix(1, 1, g * steps)
                with sp.Fori(0, QUADS // 2 - 1) as p:
                    for u in range(2):
                        load_x(q0 + p * 2 + 2 + u, u, q0 + p * 2 + u + 1)
                with sp.Fori(0, steps // 2 - 1) as p:
                    for u in range(2):
                        load_mix(p * 2 + 2 + u, u, g * steps + p * 2 + 1 + u)
                with sp.Fori(0, GI // 2) as p:
                    for u in range(2):
                        m = g * GI + p * 2 + u
                        after(sp, dve_h, m + 1)
                        sp.dma_start(h_dram[ds(m, 1)].rearrange("m (r c) h -> (m r) (c h)", r=8),
                                     h_row[0:8, u, :]).then_inc(st_h[u], 16)
            for u in range(2):
                after(sp, st_h[u], 16 * IMAGES // 2)

        @block.gpsimd
        def _(gp):
            gp.wait_ge(init_done, 3)
            with gp.Fori(0, GROUPS) as g:
                def weights(layer):
                    gl = g * LAYERS + layer
                    after(gp, pool_b, (g * (LAYERS - 1) + layer) * GI)
                    after(gp, pe_x, gl * GI)
                    gp.sem_inc(passed, 1)
                    gp.tensor_copy(conv_cur[:, :], conv_sb[:, ds(layer, 1), :].rearrange("p a b -> p (a b)")).then_inc(pool_w, 1)
                    after(gp, pool_w, gl + 1)
                    for u in range(2):
                        spread(gp, (3,), pool_spread, gl, 0, u)
                    with gp.Fori(1, MIXS // 2) as p:
                        for u in range(2):
                            spread(gp, (3,), pool_spread, gl, p, u)
                    after(gp, pool_spread, (gl + 1) * MIXS)

                with gp.Fori(0, LAYERS - 1) as layer:
                    weights(layer)
                    gp.sem_inc(passed, 1)
                    with gp.Fori(0, GI) as i:
                        after(gp, act_b, (g * LAYERS + layer) * GI + i + 1)
                        gp.sem_inc(passed, 1)
                        gp.tensor_copy(stored_b[:, ds(i, 1), :].rearrange("p a b -> p (a b)"), b_cur[:, :]).then_inc(pool_b, 1)
                weights(LAYERS - 1)

        @block.tensor
        def _(pe):
            mm = pe.matmul
            pe.wait_ge(ld_const, 16 * NCONST)
            pe.wait_ge(init_done, 3)
            pe.wait_ge(weights_split, 8)

            def transpose_pixels(v, f):
                after(pe, act_b, v + 1)
                for b in range(8):
                    last = pe.transpose(t_ps[:, b // 4, (b % 4) * 128:(b % 4 + 1) * 128], b_cur[:, b * 128:(b + 1) * 128], ident)
                last.then_inc(pe_bt, 1)

            def forward_h(v, f):
                after(pe, dve_s, f)
                after(pe, act_hi, v + 1)
                for a in range(2):
                    mm(y_ps[:, a, :], fwd_hh[:, :], pix_h[:, a * 512:(a + 1) * 512], start=True, stop=False)
                    mm(y_ps[:, a, :], fwd_hl[:, :], pix_h[:, a * 512:(a + 1) * 512], start=False, stop=False)
                after(pe, dve_lo, v + 1)
                for a in range(2):
                    last = mm(y_ps[:, a, :], fwd_hh[:, :], pix_l[:, a * 512:(a + 1) * 512], start=False, stop=True)
                last.then_inc(pe_y, 1)

            def forward_w(f):
                after(pe, dve_y, f + 1)
                y = y_sb[:, :, :].rearrange("p k c -> p (k c)")
                for k in range(KHH):
                    last = mm(s_ps[:, k * 40:(k + 1) * 40], y[:, k * 128:(k + 1) * 128], fwd_w, start=True, stop=True)
                last.then_inc(pe_s, 1)

            def transpose_spec(v, before):
                after(pe, dve_t, v + 1)
                after(pe, act_hi, before)
                after(pe, dve_lo, before)
                pe.sem_inc(passed, 1)
                for k in range(KHH):
                    last = pe.transpose(t_ps[0:120, k // 4, (k % 4) * 128:(k % 4 + 1) * 128],
                                        stage_t[:, k, :, :].rearrange("p a b -> p (a b)").bitcast(f32), ident)
                last.then_inc(pe_tt, 1)

            def inverse_w(v):
                after(pe, dve_tt, v + 1)
                after(pe, dve_u, v)
                t = tt_sb[:, :, :].rearrange("p k o -> p (k o)")
                mm(u_ps[:, 0, :], inv_w3[:, :], t[:, 0:512], start=True, stop=True)
                mm(u_ps[:, 1, 0:128], inv_w3[:, :], t[:, 512:640], start=True, stop=True).then_inc(pe_u, 1)

            def convolve(v, i):
                after(pe, act_b, v)
                for a in range(2):
                    mm(x_ps[:, a, :], conv_cur[:, :], stored_b[:, ds(i, 1), a * 512:(a + 1) * 512].rearrange("p a b -> p (a b)"),
                       start=True, stop=False, skip_group_check=True)

            def inverse_h(v):
                after(pe, dve_u, v + 1)
                for b in range(8):
                    last = mm(x_ps[:, b // 4, (b % 4) * 128:(b % 4 + 1) * 128], u_sb[:, b, :, :].rearrange("p o w -> p (o w)"), inv_h,
                              start=False, stop=b % 4 == 3, skip_group_check=True)
                last.then_inc(pe_x, 1)

            def mix(g, layer):
                gl = g * LAYERS + layer
                after(pe, dve_s, (g * (LAYERS - 1) + layer) * GI)
                after(pe, dve_lift, (g + 1) * QUADS)
                after(pe, act_b, (g * LAYERS + layer) * GI)
                after(pe, act_hi, (g * LAYERS + layer) * GI)
                after(pe, dve_lo, (g * LAYERS + layer) * GI)
                after(pe, pool_w, gl + 1)
                after(pe, act_b0, (g + 1) * QUADS * 8)
                pe.sem_inc(passed, 1)
                with pe.Fori(0, MIXS // 2) as p:
                    for u, dst in ((0, (x_ps, y_ps)), (1, (t_ps, u_ps))):
                        done = gl * (MIXS // 2) + p
                        after(pe, dve_spread, gl * MIXS + p * 2 + u + 1)
                        after(pe, pool_spread, gl * MIXS + p * 2 + u + 1)
                        after(pe, (dve_mix, act_mix)[u], done)
                        for m in range(MIXN):
                            src = spec[:, ds((p * 2 + u) * MIXN + m, 1), :, :].rearrange("p a r i -> p (a r i)")
                            for k in range(2):
                                o = dst[k][0:64].rearrange("p a b -> p (a b)")[:, m * 2 * GI:(m + 1) * 2 * GI]
                                last = mm(o, mix_slot[u][:, m, k * 64:(k + 1) * 64], src, start=True, stop=True)
                        last.then_inc(pe_mix, 1)
                after(pe, dve_mix, (gl + 1) * (MIXS // 2))

            with pe.Fori(0, GROUPS) as g:
                after(pe, act_b, g * LAYERS * GI)
                pe.wait_ge(ld_lift, g * 32 + 32)
                pe.sem_inc(passed, 1)

                def quad(q, loads, u):
                    pe.wait_ge(ld_x[u], loads)
                    pe.sem_inc(passed, 1)
                    mm(yx_ps, fwd_h, x_a[u], start=True, stop=True).then_inc(pe_yx, 1)

                    def fc0(b):
                        after(pe, act_b0, q * 8 + max(b - 1, 0))
                        pe.sem_inc(passed, 1)
                        mm(x_ps[:, b % 2, :], fc0_sb[:, b * 128:(b + 1) * 128], x_b[u], start=True, stop=True).then_inc(pe_b0, 1)

                    for b in range(4):
                        fc0(b)
                    after(pe, dve_yx, q + 1)
                    after(pe, dve_sx, q)
                    pe.sem_inc(passed, 1)
                    for i in range(Q):
                        last = mm(sx_ps[:, i * 40:(i + 1) * 40], yx_sb[:, i * 96:i * 96 + 3 * MODES], fwd_w,
                                  start=True, stop=True, skip_group_check=True)
                    last.then_inc(pe_sx, 1)
                    for b in range(4, 8):
                        fc0(b)
                    after(pe, dve_sx, q + 1)
                    after(pe, dve_lift, q)
                    pe.sem_inc(passed, 1)
                    for k in range(KHH):
                        last = mm(t_ps[:, k // 3, k % 3 * 160:(k % 3 + 1) * 160], lift_sb[:, k * 128:(k + 1) * 128], sx_sb,
                                  start=True, stop=True, skip_group_check=True)
                    last.then_inc(pe_lift, 1)

                with pe.Fori(0, QUADS // 2) as p:
                    for u in range(2):
                        quad(g * QUADS + p * 2 + u, (g * (QUADS // 2) + p) * 32 + 32, u)

                with pe.Fori(0, LAYERS - 1) as layer:
                    mix(g, layer)
                    v0, f0 = (g * LAYERS + layer) * GI, (g * (LAYERS - 1) + layer) * GI
                    after(pe, pool_b, f0)
                    convolve(v0, 0)
                    after(pe, act_mix, (g * LAYERS + layer + 1) * (MIXS // 2))
                    transpose_spec(v0, v0)
                    inverse_w(v0)

                    def layer_pass(i, prev, u, first, last):
                        v, f = v0 + i, f0 + i
                        inverse_h(v)
                        if not first:
                            forward_h(v0 + prev, f0 + prev)
                        if not last:
                            transpose_spec(v + 1, v)
                            convolve(v + 1, i + 1)
                            inverse_w(v + 1)
                        transpose_pixels(v, f)
                        if not first:
                            forward_w(f0 + prev)

                    image_loop(pe, layer_pass)
                    forward_h(v0 + GI - 1, f0 + GI - 1)
                    forward_w(f0 + GI - 1)

                mix(g, LAYERS - 1)
                v0 = (g * LAYERS + LAYERS - 1) * GI
                f_all = (g + 1) * (LAYERS - 1) * GI
                after(pe, pool_b, f_all)
                convolve(v0, 0)
                after(pe, act_mix, (g + 1) * LAYERS * (MIXS // 2))
                transpose_spec(v0, v0)
                inverse_w(v0)

                def fc1(m, c, v):
                    if c >= 2:
                        after(pe, act_g, m * 4 + c - 1)
                    half = slice((c // 2) * 512, (c // 2 + 1) * 512)
                    mm(y_ps[:, c % 2, :], fc1_h[:, c % 2, :], pix_h[:, half], start=True, stop=False)
                    mm(y_ps[:, c % 2, :], fc1_l[:, c % 2, :], pix_h[:, half], start=False, stop=False)
                    if c == 0:
                        after(pe, dve_lo, v + 1)
                    mm(y_ps[:, c % 2, :], fc1_h[:, c % 2, :], pix_l[:, half], start=False, stop=True).then_inc(pe_fc1, 1)

                def fc2(m, c):
                    after(pe, act_g, m * 4 + c + 1)
                    mm(h_ps, fc2_sb[:, c, :], g_sb[:, c % 2, :], start=c == 0, stop=c == 3).then_inc(pe_fc2, 1)

                def last_pass(i, prev, u, first, last):
                    v = v0 + i
                    inverse_h(v)
                    if not first:
                        m = g * GI + prev
                        after(pe, act_hi, v0 + prev + 1)
                        fc1(m, 0, v0 + prev)
                        fc1(m, 1, v0 + prev)
                    if not last:
                        after(pe, dve_h, g * GI + (0 if first else prev))
                        transpose_spec(v + 1, v0)
                        convolve(v + 1, i + 1)
                        inverse_w(v + 1)
                    if not first:
                        if last:
                            after(pe, dve_h, m)
                        fc2(m, 0)
                        fc1(m, 2, v0 + prev)
                        fc2(m, 1)
                        fc1(m, 3, v0 + prev)
                    if not first:
                        fc2(m, 2)
                        fc2(m, 3)

                image_loop(pe, last_pass)
                m = g * GI + GI - 1
                after(pe, act_hi, v0 + GI)
                fc1(m, 0, v0 + GI - 1)
                fc1(m, 1, v0 + GI - 1)
                after(pe, dve_h, m)
                fc2(m, 0)
                fc1(m, 2, v0 + GI - 1)
                fc2(m, 1)
                fc1(m, 3, v0 + GI - 1)
                fc2(m, 2)
                fc2(m, 3)
                after(pe, dve_h, g * GI + GI)

        @block.scalar
        def _(act):
            x_f = x_ps.rearrange("p a b -> p (a b)")
            t_f = t_ps.rearrange("p a b -> p (a b)")
            act.wait_ge(ld_const, 16 * NCONST)

            def gelu(v, dst):
                after(act, pe_x, v + 1)
                act.activation(dst, x_f, ACT.Gelu).then_inc(act_b, 1)

            with act.Fori(0, GROUPS) as g:
                with act.Fori(0, QUADS // 2) as p:
                    for b in range(16):
                        after(act, pe_b0, (g * QUADS + p * 2) * 8 + b + 1)
                        act.activation(stored_b[:, ds((p * 2 + b // 8) * Q, Q), b % 8 * 128:(b % 8 + 1) * 128],
                                       x_ps[:, b % 2, :].rearrange("p (i f) -> p i f", i=Q), ACT.Copy).then_inc(act_b0, 1)

                def mix_evac(layer):
                    gl = g * LAYERS + layer
                    act.activation(table[:, :], fc1b_sb[:, :], ACT.Gelu)
                    for p in range(MIXS // 2):
                        after(act, pe_mix, gl * MIXS + p * 2 + 2)
                        for k, src in enumerate((t_ps, u_ps)):
                            dst = spec[k * 64:(k + 1) * 64, ds((p * 2 + 1) * MIXN, MIXN), :, :].rearrange("p m r i -> p (m r i)")
                            last = act.activation(dst, src[0:64].rearrange("p a b -> p (a b)")[:, 0:MF], ACT.Copy)
                        last.then_inc(act_mix, 1)

                with act.Fori(0, LAYERS - 1) as layer:
                    mix_evac(layer)

                    def layer_pass(i, prev, u, first, last):
                        f = (g * (LAYERS - 1) + layer) * GI + i
                        after(act, pe_bt, f)
                        after(act, pool_b, f)
                        gelu((g * LAYERS + layer) * GI + i, b_cur[:, :])
                        after(act, pe_bt, f + 1)
                        after(act, pe_y, f)
                        act.activation(pix_h[:, :], t_f, ACT.Copy).then_inc(act_hi, 1)

                    image_loop(act, layer_pass)
                mix_evac(LAYERS - 1)
                after(act, pe_bt, (g + 1) * (LAYERS - 1) * GI)
                after(act, pool_b, (g + 1) * (LAYERS - 1) * GI)
                after(act, pe_y, (g + 1) * (LAYERS - 1) * GI)

                def head(m):
                    for c in range(4):
                        after(act, pe_fc1, m * 4 + c + 1)
                        after(act, pe_fc2, m * 4 + c - 1 if c >= 2 else m * 4)
                        act.activation(g_sb[:, c % 2, :], y_ps[:, c % 2, :], ACT.Gelu, bias=fc1b_sb[:, :]).then_inc(act_g, 1)

                def last_pass(i, prev, u, first, last):
                    v = (g * LAYERS + LAYERS - 1) * GI + i
                    after(act, dve_lo, v)
                    gelu(v, b_cur[:, :])
                    if not first:
                        head(g * GI + prev)
                    after(act, act_b, v + 1)
                    act.activation(pix_h[:, :], b_cur[:, :], ACT.Copy).then_inc(act_hi, 1)

                image_loop(act, last_pass)
                head(g * GI + GI - 1)

        @block.vector
        def _(dve):
            dve.memset(u_ps, 0.0).then_inc(init_done, 1)
            dve.wait_ge(ld_const, 16 * NCONST)
            dve.tensor_scalar(convb_sb[:, :], convb_raw[:, :], float(H * W) ** 0.5, None, ALU.mult).then_inc(dve_cb, 1)
            after(dve, dve_cb, 1)
            for u in range(2):
                dve.memset(mix_slot[u][:, :, :], 0.0).then_inc(init_done, 1)
            dve.wait_ge(init_done, 3)

            rounded, rest, low = (spec[0:120, 2 * k:2 * k + 2, :, :].rearrange("p a b c -> p (a b c)") for k in range(3))
            rounded = rounded.bitcast(f32r)
            dve.tensor_copy(rounded, inv_w).then_inc(weights_split, 1)
            dve.wait_ge(weights_split, 1)
            dve.tensor_tensor(rest, inv_w, rounded.bitcast(f32), ALU.subtract).then_inc(weights_split, 1)
            dve.wait_ge(weights_split, 2)
            dve.tensor_scalar(low, rest, in_low, None, ALU.mult).then_inc(weights_split, 1)
            dve.wait_ge(weights_split, 3)
            dve.scalar_tensor_tensor(inv_w3[:, :], rounded.bitcast(f32), in_high, low, ALU.mult, ALU.add).then_inc(weights_split, 1)
            dve.wait_ge(weights_split, 4)
            dve.tensor_copy(fwd_hh[:, :], fwd_h).then_inc(weights_split, 1)
            dve.wait_ge(weights_split, 5)
            dve.tensor_tensor(fwd_hl[:, :], fwd_h, fwd_hh[:, :].bitcast(f32), ALU.subtract).then_inc(weights_split, 1)
            dve.tensor_copy(fc1_h[:, :, :], fc1_sb[:, :, :]).then_inc(weights_split, 1)
            dve.wait_ge(weights_split, 7)
            dve.tensor_tensor(fc1_l[:, :, :], fc1_sb[:, :, :], fc1_h[:, :, :].bitcast(f32), ALU.subtract).then_inc(weights_split, 1)

            t_f = t_ps.rearrange("p a b -> p (a b)")

            def stage_spec(v, i):
                after(dve, pe_tt, v)
                src = spec[:, :, :, ds(i, 1)].rearrange("p (a k) r c -> p a (k r c)", a=KHH)
                for part in (0, 2):
                    dve.tensor_copy(stage_t[:, :, part, :], src).then_inc(dve_high, 1)
                after(dve, dve_high, 2 * v + 2)
                dve.tensor_tensor(stage_t[:, :, 1, :], src, stage_t[:, :, 0, :].bitcast(f32), ALU.subtract).then_inc(dve_t, 1)

            def copy_tt(v):
                after(dve, pe_tt, v + 1)
                after(dve, pe_u, v)
                dve.tensor_copy(tt_sb[:, :, :].rearrange("p k o -> p (k o)"),
                                t_ps[0:120].rearrange("p a b -> p (a b)")[:, 0:640]).then_inc(dve_tt, 1)

            def turn_u(v, n):
                after(dve, pe_u, v + 1)
                after(dve, pe_x, n)
                src = u_ps.rearrange("p a (k o) -> p o (a k)", o=C)
                dve.transpose(u_sb[:, :, :, :].rearrange("p b o w -> p o b w"), src).then_inc(dve_u, 1)

            def split_pixels(v, src, s, n):
                after(dve, act_hi, v + 1)
                after(dve, s, n)
                dve.tensor_tensor(pix_l[:, :], src, pix_h[:, :].bitcast(f32), ALU.subtract).then_inc(dve_lo, 1)

            def turn_y(f):
                after(dve, pe_y, f + 1)
                after(dve, pe_s, f)
                src = y_ps.rearrange("p a (b c w) -> p c (a b) w", b=4, w=4)
                dve.transpose(y_sb[:, :, :].rearrange("p k c -> p c k"), src).then_inc(dve_y, 1)

            def keep_spec(f, i):
                after(dve, pe_s, f + 1)
                dve.sem_inc(passed, 1)
                dve.tensor_copy(spec[:, :, :, ds(i, 1)].rearrange("p a b c -> p (a b c)"), s_ps).then_inc(dve_s, 1)

            with dve.Fori(0, GROUPS) as g:
                for rows, cols, v in ((slice(0, 97), slice(0, Q * 40), 0.0),
                                      (slice(96, 97), slice(0, Q * 40, 40), float(H * W) ** 0.5)):
                    dve.memset(sx_sb[rows, cols], v).then_inc(dve_bias, 1)
                    dve.wait_ge(dve_bias, g * 2 + (1 if v == 0.0 else 2))
                dve.sem_inc(passed, 1)

                for u in range(2):
                    spread(dve, range(3), dve_spread, g * LAYERS, 0, u)

                with dve.Fori(0, QUADS) as p:
                    q = g * QUADS + p
                    after(dve, pe_yx, q + 1)
                    after(dve, pe_sx, q)
                    for i in range(Q):
                        last = dve.transpose(yx_sb[:, i * 96:(i + 1) * 96].rearrange("p (k m) -> p m k", m=3),
                                             yx_ps[:, i * 96:(i + 1) * 96].rearrange("p (m w) -> p m w", w=WL))
                    last.then_inc(dve_yx, 1)
                    after(dve, pe_sx, q + 1)
                    after(dve, pe_lift, q)
                    dve.tensor_copy(sx_sb[0:3 * MODES, :], sx_ps).then_inc(dve_sx, 1)
                    after(dve, pe_lift, q + 1)
                    for k, n in ((0, 3), (3, 2)):
                        last = dve.tensor_copy(
                            spec[:, k * MODES:(k + n) * MODES, :, ds(p * Q, Q)].rearrange("p (a k) r i -> p a i (k r)", a=n),
                            t_ps[:, k // 3, 0:n * 160].rearrange("p (a i m) -> p a i m", a=n, i=Q))
                    last.then_inc(dve_lift, 1)

                def mix_evac(layer):
                    gl = g * LAYERS + layer

                    def keep(p):
                        after(dve, pe_mix, gl * MIXS + p * 2 + 1)
                        for k, src in enumerate((x_ps, y_ps)):
                            dst = spec[k * 64:(k + 1) * 64, ds((p * 2) * MIXN, MIXN), :, :].rearrange("p m r i -> p (m r i)")
                            last = dve.tensor_copy(dst, src[0:64].rearrange("p a b -> p (a b)")[:, 0:MF])
                        last.then_inc(dve_mix, 1)

                    with dve.Fori(0, MIXS // 2 - 1) as p:
                        spread(dve, range(3), dve_spread, gl, p + 1, 0)
                        keep(p)
                        spread(dve, range(3), dve_spread, gl, p + 1, 1)
                    keep(MIXS // 2 - 1)
                    after(dve, dve_mix, (gl + 1) * (MIXS // 2))
                    mode0 = spec[0:C, 0, 0, :]
                    dve.tensor_tensor(mode0, mode0, convb_sb[:, ds(layer, 1)].to_broadcast([C, GI]), ALU.add).then_inc(dve_cb, 1)
                    after(dve, dve_cb, gl + 2)
                    after(dve, act_mix, (gl + 1) * (MIXS // 2))

                with dve.Fori(0, LAYERS - 1) as layer:
                    mix_evac(layer)
                    v0, f0 = (g * LAYERS + layer) * GI, (g * (LAYERS - 1) + layer) * GI
                    stage_spec(v0, 0)
                    copy_tt(v0)
                    turn_u(v0, v0)

                    def layer_pass(i, prev, u, first, last):
                        if not first:
                            split_pixels(v0 + prev, t_f, pe_y, f0 + prev)
                        if not last:
                            stage_spec(v0 + i + 1, i + 1)
                        if not first:
                            turn_y(f0 + prev)
                        if not last:
                            copy_tt(v0 + i + 1)
                            turn_u(v0 + i + 1, v0 + i + 1)
                        if not first:
                            keep_spec(f0 + prev, prev)

                    image_loop(dve, layer_pass)
                    split_pixels(v0 + GI - 1, t_f, pe_y, f0 + GI - 1)
                    turn_y(f0 + GI - 1)
                    for k in range(2):
                        spread(dve, range(3), dve_spread, g * LAYERS + layer + 1, 0, k)
                    keep_spec(f0 + GI - 1, GI - 1)

                mix_evac(LAYERS - 1)
                v0 = (g * LAYERS + LAYERS - 1) * GI
                stage_spec(v0, 0)
                copy_tt(v0)
                turn_u(v0, v0)

                def keep_h(m, u):
                    after(dve, pe_fc2, (m + 1) * 4)
                    after(dve, st_h[u], (m - u) * 8)
                    dve.tensor_scalar(h_row[0:8, u, :], h_ps, fc2b_sb[:, :], None, ALU.add).then_inc(dve_h, 1)

                def last_pass(i, prev, u, first, last):
                    if not last:
                        stage_spec(v0 + i + 1, i + 1)
                        copy_tt(v0 + i + 1)
                        turn_u(v0 + i + 1, v0 + i + 1)
                    split_pixels(v0 + i, b_cur[:, :], pe_fc1, (g * GI + i) * 4)
                    if not first:
                        keep_h(g * GI + prev, 1 - u)

                image_loop(dve, last_pass)
                keep_h(g * GI + GI - 1, (GI - 1) % 2)


def attention_and_experts(nc, h_dram, attn_w, moe_w1, moe_b1, moe_w2, moe_b2, gate_w, gate_b, selector, eye,
                          column_order, ln_gb, out):
    f32, f32r, u32 = mybir.dt.float32, mybir.dt.float32r, mybir.dt.uint32
    ALU, ACT, AX = mybir.AluOpType, mybir.ActivationFunctionType, mybir.AxisListType
    ds = bass.ds

    with ExitStack() as ctx:
        def sb(name, shape, dt=f32):
            return ctx.enter_context(nc.sbuf_tensor(name, shape, dt))

        def sem(name):
            return ctx.enter_context(nc.semaphore(name))

        h_in = sb("h_in", [D, CH])
        tok_h = sb("tok_h", [128, CT, D])
        centred = sb("centred", [128, CT, D])
        squares = sb("squares", [128, CT, D])
        tok_n = sb("tok_n", [128, CT, D])
        xt = sb("xt", [D + 1, CH])
        q_t = sb("q_t", [D, CH])
        k_t = sb("k_t", [D, CH])
        v_sb = sb("v_sb", [128, CT, D + 2])
        score = sb("score", [128, CT, H])
        prob_bd = sb("prob_bd", [128, CT, 128])
        prob_t = sb("prob_t", [128, CT, 128])
        o_t = sb("o_t", [D + 1, CH])
        tok_h2 = sb("tok_h2", [128, CT, D])
        tok_n2 = sb("tok_n2", [128, CT, D])
        n2_hl = sb("n2_hl", [128, CT, 2, D], f32r)
        x_hl = sb("x_hl", [128, CH], f32r)
        logit = sb("logit", [128, CT, E])
        top8 = sb("top8", [128, CT, 8])
        idx_u = sb("idx_u", [128, CT, 8], u32)
        idx_f = sb("idx_f", [128, CT, 8])
        iota_u = sb("iota_u", [128, E], mybir.dt.int32)
        iota_f = sb("iota_f", [128, E])
        oh1 = sb("oh1", [128, CT, E])
        oh2 = sb("oh2", [128, CT, E])
        gate = sb("gate", [128, CT, E])
        gate_hl = sb("gate_hl", [128, CT, 2, E], f32r)
        gate_t = sb("gate_t", [2 * E, CH], f32r)
        relu = [sb(f"relu{u}", [128, HALF]) for u in range(3)]
        gated = [sb(f"gated{u}", [128, HALF]) for u in range(3)]
        gated_h = [sb(f"gated_h{u}", [128, HALF], f32r) for u in range(3)]
        gated_l = [sb(f"gated_l{u}", [128, HALF], f32r) for u in range(3)]
        z_sb = sb("z_sb", [128, CH])
        acc1 = sb("acc1", [128, CT, D])
        acc2 = sb("acc2", [128, CT, D])
        tok_o = sb("tok_o", [128, CT, D])
        stat = sb("stat", [128, 14, CT])
        attn_sb = sb("attn_sb", [D + 1, 4 * D + 2])
        ident = sb("ident", [128, 128])
        order = sb("order", [D, D])
        gate_sb = sb("gate_sb", [128, E])
        gateb_sb = sb("gateb_sb", [128, E])
        gb_sb = sb("gb_sb", [128, 2, D])
        b1_sb = sb("b1_sb", [128, E])
        w1_raw = sb("w1_raw", [128, E, F])
        w2_raw = sb("w2_raw", [128, E, D])
        b2_raw = sb("b2_raw", [2 * E, D])
        sel_raw = sb("sel_raw", [2 * E, E, 128])
        w1_h = sb("w1_h", [128, E, F], f32r)
        w1_l = sb("w1_l", [128, E, F], f32r)
        w2_hl = sb("w2_hl", [128, E, 2, D], f32r)
        b2_hl = sb("b2_hl", [2 * E, 2, D], f32r)
        sel = sb("sel", [2 * E, E, 128], f32r)

        bank = ctx.enter_context(nc.psum_tensor("bank", [128, 8, 512], f32))

        ld_attn, ld_moe, ld_tok = sem("ld_attn"), sem("ld_moe"), sem("ld_tok")
        st_out = sem("st_out")
        weights_cut, tail_init = sem("weights_cut"), sem("tail_init")
        t_pe, t_act, t_dve = ([sem(f"t_{n}{s}") for s in range(2)] for n in ("pe", "act", "dve"))
        up_done, relu_done, gated_done = sem("up_done"), sem("relu_done"), sem("gated_done")
        high_done, low_done, down_done = sem("high_done"), sem("low_done"), sem("down_done")
        counted = [st_out]
        tail_passed = sem("tail_passed")

        NATTN, NMOE = 4, 7
        moe_loads = ((gate_sb, gate_w), (gateb_sb, gate_b.to_broadcast([128, E])), (b1_sb, moe_b1), (b2_raw, moe_b2),
                     (sel_raw, selector), (w1_raw, moe_w1), (w2_raw, moe_w2))
        block = ctx.enter_context(nc.Block())

        UP_BANK, GATE_BANK = (0, 1, 6), (2, 3, 7)
        HT = CT // 2
        TILES = [range(s * HT, (s + 1) * HT) for s in range(2)]
        PART = [slice(s * HT, (s + 1) * HT) for s in range(2)]
        COLS = [slice(s * HALF, (s + 1) * HALF) for s in range(2)]

        def whole(t):
            names = " ".join("abc"[:len(t.shape) - 1])
            return t[tuple([slice(None)] * len(t.shape))].rearrange(f"p {names} -> p ({names})") if len(t.shape) > 2 else t[:, :]

        @block.sync
        def _(sp):
            for s in counted:
                sp.sem_inc(s, 1)
            def load(c):
                sp.dma_start(h_in[:, :].rearrange("w (b h) -> w b h", h=H),
                             h_dram[ds(c * (CH // H), CH // H)].rearrange("b w h -> w b h")).then_inc(ld_tok, 16)

            out_rows = out.rearrange("b h w -> (b h) w").rearrange("(c t p) w -> c p t w", t=CT, p=128)
            load(0)
            for dst, src in ((ident[:, :], eye), (order[:, :], column_order), (attn_sb[:, :], attn_w),
                             (gb_sb[:, :, :], ln_gb.rearrange("(o a) d -> o a d", o=1).to_broadcast([128, 2, D]))):
                sp.dma_start(dst, src).then_inc(ld_attn, 16)
            for dst, src in moe_loads:
                sp.dma_start(whole(dst), src).then_inc(ld_moe, 16)

            def store(c):
                for s in range(2):
                    sp.wait_ge(t_dve[s], STEPS["dve"] * (c + 1))
                sp.dma_start(out_rows[ds(c, 1)].rearrange("c p t w -> p (c t) w"), tok_o[:, :, :]).then_inc(st_out, 16)

            with sp.Fori(0, TOK // CH - 1) as c:
                for s in range(2):
                    sp.wait_ge(t_pe[s], c * STEPS["pe"] + 1)
                load(c + 1)
                store(c)
            store(TOK // CH - 1)
            sp.wait_ge(st_out, 1 + 16 * (TOK // CH))

        @block.gpsimd
        def _(gp):
            gp.iota(iota_u[:, :], pattern=[[1, E]], base=0, channel_multiplier=0).then_inc(tail_init, 1)
            gp.wait_ge(ld_moe, 16 * NMOE)
            gp.tensor_copy(whole(sel), whole(sel_raw)).then_inc(weights_cut, 1)
            gp.tensor_copy(b2_hl[:, 0, :], b2_raw[:, :]).then_inc(weights_cut, 1)
            gp.tensor_copy(whole(w1_h), whole(w1_raw)).then_inc(weights_cut, 1)
            gp.tensor_copy(w2_hl[:, :, 0, :], w2_raw[:, :, :]).then_inc(weights_cut, 1)
            gp.wait_ge(weights_cut, 4)
            gp.tensor_tensor(b2_hl[:, 1, :], b2_raw[:, :], b2_hl[:, 0, :].bitcast(f32), ALU.subtract).then_inc(weights_cut, 1)
            gp.tensor_tensor(whole(w1_l), whole(w1_raw), whole(w1_h).bitcast(f32), ALU.subtract).then_inc(weights_cut, 1)
            gp.tensor_tensor(w2_hl[:, :, 1, :], w2_raw[:, :, :], w2_hl[:, :, 0, :].bitcast(f32),
                             ALU.subtract).then_inc(weights_cut, 1)

        @block.tensor
        def _(pe):
            mm = pe.matmul
            pe.wait_ge(ld_attn, 16 * NATTN)
            pe.wait_ge(tail_init, 4)
            with pe.Fori(0, TOK // CH) as c:
                def when(s, k, total):
                    pe.wait_ge(s, c * total + k)

                nd, na, steps = STEPS["dve"], STEPS["act"], EXPERT_STEPS

                def cols(t):
                    return slice(t % HT * 128, (t % HT + 1) * 128)

                def tok(t):
                    return slice(t * 128, (t + 1) * 128)

                pe.wait_ge(ld_tok, c * 16 + 16)
                pe.sem_inc(tail_passed, 1)
                for s in range(2):
                    for t in TILES[s]:
                        last = mm(bank[:, 4 + s, t % HT * D:(t % HT + 1) * D], h_in[:, tok(t)], order[:, :],
                                  start=True, stop=True, skip_group_check=True)
                    last.then_inc(t_pe[s], 1)
                for s in range(2):
                    when(t_dve[s], PLACE["n1"], nd)
                    pe.sem_inc(tail_passed, 1)
                    for t in TILES[s]:
                        last = pe.transpose(bank[0:D, s, cols(t)], tok_n[:, t, :], ident[:, :])
                    last.then_inc(t_pe[s], 1)
                for s in range(2):
                    when(t_act[s], 3, na)
                    for j, b in ((0, 2), (1, 4)):
                        mm(bank[0:D, b + s, :], attn_sb[:, j * D:(j + 1) * D], xt[:, COLS[s]],
                           start=True, stop=True).then_inc(t_pe[s], 1)
                    for t in TILES[s]:
                        last = mm(bank[:, 6 + s, t % HT * 66:(t % HT + 1) * 66], xt[:, tok(t)],
                                  attn_sb[:, 2 * D:3 * D + 2], start=True, stop=True, skip_group_check=True)
                    last.then_inc(t_pe[s], 1)
                for s in range(2):
                    when(t_act[s], 4, na)
                    when(t_dve[s], PLACE["k"], nd)
                    pe.sem_inc(tail_passed, 1)
                    for t in TILES[s]:
                        for b in range(2):
                            tk = slice(t * 128 + b * 64, t * 128 + b * 64 + 64)
                            last = mm(bank[b * 64:(b + 1) * 64, s, t % HT * H:(t % HT + 1) * H], q_t[:, tk], k_t[:, tk],
                                      start=True, stop=True, skip_group_check=True)
                    last.then_inc(t_pe[s], 1)
                for s in range(2):
                    when(t_dve[s], PLACE["p"], nd)
                    for t in TILES[s]:
                        last = pe.transpose(bank[:, 2 + s, cols(t)], prob_bd[:, t, :], ident[:, :])
                    last.then_inc(t_pe[s], 1)
                for s in range(2):
                    when(t_act[s], 7, na)
                    for t in TILES[s]:
                        last = mm(bank[0:D, 4 + s, cols(t)], v_sb[:, t, 0:D], prob_t[:, t, :],
                                  start=True, stop=True, skip_group_check=True)
                    last.then_inc(t_pe[s], 1)
                for s in range(2):
                    when(t_dve[s], PLACE["o"], nd)
                    for t in TILES[s]:
                        last = mm(bank[:, 6 + s, t % HT * D:(t % HT + 1) * D], o_t[:, tok(t)], attn_sb[:, 3 * D + 2:4 * D + 2],
                                  start=True, stop=True, skip_group_check=True)
                    last.then_inc(t_pe[s], 1)
                for s in range(2):
                    when(t_dve[s], PLACE["n2_hl"], nd)
                    for t in TILES[s]:
                        last = pe.transpose(bank[:, s, cols(t)],
                                            n2_hl[:, t, :, :].rearrange("p a d -> p (a d)").bitcast(f32), ident[:, :])
                    last.then_inc(t_pe[s], 1)
                pe.wait_ge(ld_moe, 16 * NMOE)
                for s in range(2):
                    when(t_act[s], 9, na)
                    for t in TILES[s]:
                        last = mm(bank[:, 2 + s, t % HT * E:(t % HT + 1) * E], x_hl[:, tok(t)].bitcast(f32), gate_sb[:, :],
                                  start=True, stop=True, skip_group_check=True)
                    last.then_inc(t_pe[s], 1)
                for s in range(2):
                    when(t_dve[s], PLACE["g"], nd)
                    for t in TILES[s]:
                        last = pe.transpose(bank[0:2 * E, 4 + s, cols(t)],
                                            gate_hl[:, t, :, :].rearrange("p a e -> p (a e)").bitcast(f32), ident[:, :])
                    last.then_inc(t_pe[s], 1)
                pe.wait_ge(weights_cut, 7)

                def up(k):
                    half, e = k // E, k % E
                    toks = slice(half * HALF, (half + 1) * HALF)
                    if k >= 3:
                        pe.wait_ge(relu_done, c * steps + k - 2)
                    mm(bank[:, UP_BANK[k % 3], :], w1_h[:, e, :], x_hl[:, toks], start=True, stop=False)
                    mm(bank[:, UP_BANK[k % 3], :], w1_l[:, e, :], x_hl[:, toks], start=False, stop=True)
                    if k == 0:
                        when(t_act[0], 11, na)
                        when(t_act[1], 11, na)
                    if k >= 3:
                        pe.wait_ge(gated_done, c * steps + k - 2)
                    mm(bank[:, GATE_BANK[k % 3], :], sel[:, e, :], gate_t[:, toks], start=True, stop=True).then_inc(up_done, 1)

                def down(k):
                    half, e = k // E, k % E
                    z = bank[:, 4 + half, :]
                    if e == 0:
                        mm(z, b2_hl[:, :, :].rearrange("p a d -> p (a d)"), gate_t[:, half * HALF:(half + 1) * HALF],
                           start=True, stop=False)
                    w2 = w2_hl[:, e, :, :].rearrange("p a d -> p (a d)")
                    pe.wait_ge(high_done, c * steps + k + 1)
                    mm(z, w2, gated_h[k % 3][:, :], start=False, stop=False)
                    pe.wait_ge(low_done, c * steps + k + 1)
                    mm(z, w2, gated_l[k % 3][:, :], start=False, stop=e == E - 1).then_inc(down_done, 1)

                up(0)
                up(1)
                up(2)
                for k in range(steps):
                    if k + 3 < steps:
                        up(k + 3)
                    down(k)
                for s in range(2):
                    when(t_act[s], 12, na)
                    for t in TILES[s]:
                        last = pe.transpose(bank[:, s, cols(t)], z_sb[:, tok(t)], ident[:, :])
                    last.then_inc(t_pe[s], 1)

        @block.scalar
        def _(act):
            act.wait_ge(ld_moe, 16 * NMOE)
            with act.Fori(0, TOK // CH) as c:
                def when(s, k, total):
                    act.wait_ge(s, c * total + k)

                npe, nd, steps = STEPS["pe"], STEPS["dve"], EXPERT_STEPS

                def flat(v):
                    return v.rearrange("p a b -> p (a b)")

                def root(name):
                    for s in range(2):
                        when(t_dve[s], PLACE[name], nd)
                        act.activation(stat[:, 4, PART[s]], stat[:, 3, PART[s]], ACT.Sqrt).then_inc(t_act[s], 1)

                def copy(dst, src, step):
                    for s in range(2):
                        when(t_pe[s], step, npe)
                        act.activation(dst(s), src(s), ACT.Copy).then_inc(t_act[s], 1)

                copy(lambda s: flat(tok_h[:, PART[s], :]), lambda s: bank[:, 4 + s, 0:HT * D], 1)
                root("var1")
                copy(lambda s: xt[0:D, COLS[s]], lambda s: bank[0:D, s, :], 2)
                copy(lambda s: q_t[:, COLS[s]], lambda s: bank[0:D, 2 + s, :], 3)
                copy(lambda s: flat(v_sb[:, PART[s], :]), lambda s: bank[:, 6 + s, 0:HT * 66], 5)
                for s in range(2):
                    when(t_dve[s], PLACE["sub"], nd)
                    act.activation(flat(score[:, PART[s], :]), flat(score[:, PART[s], :]), ACT.Exp,
                                   scale=float(D) ** -0.5).then_inc(t_act[s], 1)
                copy(lambda s: flat(prob_t[:, PART[s], :]), lambda s: bank[:, 2 + s, :], 7)
                root("var2")
                copy(lambda s: x_hl[:, COLS[s]], lambda s: bank[:, s, :], 10)
                for s in range(2):
                    when(t_dve[s], PLACE["diff"], nd)
                    act.activation(stat[:, 8, PART[s]], stat[:, 7, PART[s]], ACT.Exp).then_inc(t_act[s], 1)
                copy(lambda s: gate_t[:, COLS[s]], lambda s: bank[0:2 * E, 4 + s, :], 12)

                def rectify(k):
                    act.wait_ge(up_done, c * steps + k + 1)
                    if k >= 3:
                        act.wait_ge(gated_done, c * steps + k - 2)
                    act.activation(relu[k % 3][:, :], bank[:, UP_BANK[k % 3], :], ACT.Relu,
                                   bias=b1_sb[:, k % E:k % E + 1]).then_inc(relu_done, 1)

                def high(k):
                    act.wait_ge(gated_done, c * steps + k + 1)
                    if k >= 3:
                        act.wait_ge(down_done, c * steps + k - 2)
                    act.activation(gated_h[k % 3][:, :], gated[k % 3][:, :], ACT.Copy).then_inc(high_done, 1)

                rectify(0)
                for k in range(steps):
                    if k + 1 < steps:
                        rectify(k + 1)
                    high(k)
                act.wait_ge(down_done, c * steps + steps)
                for s in range(2):
                    act.activation(z_sb[:, COLS[s]], bank[:, 4 + s, :], ACT.Copy).then_inc(t_act[s], 1)
                root("var3")

        @block.vector
        def _(dve):
            dve.memset(prob_bd[:, :, :], 0.0).then_inc(tail_init, 1)
            dve.memset(xt[D:D + 1, :], 1.0).then_inc(tail_init, 1)
            dve.memset(o_t[D:D + 1, :], 1.0).then_inc(tail_init, 1)
            dve.wait_ge(tail_init, 4)
            dve.tensor_copy(iota_f[:, :], iota_u[:, :]).then_inc(tail_init, 1)
            dve.wait_ge(tail_init, 5)
            dve.wait_ge(ld_attn, 16 * NATTN)
            with dve.Fori(0, TOK // CH) as c:
                nd, npe, na, steps = STEPS["dve"], STEPS["pe"], STEPS["act"], EXPERT_STEPS
                count = [0, 0]

                def settled(s):
                    dve.wait_ge(t_dve[s], c * nd + count[s])

                def done(s, ins, name=None):
                    count[s] += 1
                    assert name is None or PLACE[name] == count[s], (name, count)
                    ins.then_inc(t_dve[s], 1)

                def when(s, k, total):
                    dve.wait_ge(s, c * total + k)

                def row(s, k):
                    return stat[:, k, PART[s]]

                def wide(v, n=D):
                    return v.unsqueeze(2).to_broadcast([128, HT, n])

                def tiles(s, b):
                    return bank[:, b + s, 0:HT * D].rearrange("p (t d) -> p t d", t=HT)

                def norm(dst, src, k, name=None):
                    for s in range(2):
                        if k == 1:
                            when(t_act[s], 1, na)
                        else:
                            settled(s)
                        done(s, dve.tensor_reduce(row(s, 0), src[:, PART[s], :], AX.X, ALU.add))
                    for s in range(2):
                        settled(s)
                        done(s, dve.scalar_tensor_tensor(centred[:, PART[s], :], wide(row(s, 0)), -1.0 / D, src[:, PART[s], :],
                                                         ALU.mult, ALU.add))
                    for s in range(2):
                        settled(s)
                        done(s, dve.tensor_tensor(squares[:, PART[s], :], centred[:, PART[s], :], centred[:, PART[s], :], ALU.mult))
                    for s in range(2):
                        settled(s)
                        done(s, dve.tensor_reduce(row(s, 2), squares[:, PART[s], :], AX.X, ALU.add))
                    for s in range(2):
                        settled(s)
                        done(s, dve.tensor_scalar(row(s, 3), row(s, 2), 1.0 / D, EPS, ALU.mult, ALU.add), f"var{k}")
                    for s in range(2):
                        when(t_act[s], (2, 8, 13)[k - 1], na)
                        done(s, dve.reciprocal(row(s, 12), row(s, 4)))
                    for s in range(2):
                        settled(s)
                        done(s, dve.tensor_tensor(dst[:, PART[s], :], centred[:, PART[s], :], wide(row(s, 12)), ALU.mult), name)

                norm(tok_n, tok_h, 1, "n1")
                for s in range(2):
                    when(t_pe[s], 4, npe)
                    done(s, dve.tensor_copy(k_t[:, COLS[s]], bank[0:D, 4 + s, :]), "k")
                for s in range(2):
                    when(t_act[s], 5, na)
                    done(s, dve.tensor_scalar(row(s, 5), v_sb[:, PART[s], D], 0.0, None, ALU.not_equal))
                    done(s, dve.tensor_scalar(row(s, 6), v_sb[:, PART[s], D + 1], 0.0, None, ALU.not_equal))
                for s in range(2):
                    settled(s)
                    done(s, dve.tensor_tensor(row(s, 13), row(s, 5), row(s, 6), ALU.mult))
                for s in range(2):
                    when(t_pe[s], 6, npe)
                    done(s, dve.tensor_reduce(row(s, 9), tiles(s, 0), AX.X, ALU.max))
                for s in range(2):
                    settled(s)
                    done(s, dve.tensor_tensor(score[:, PART[s], :], tiles(s, 0), wide(row(s, 9), H), ALU.subtract), "sub")
                for s in range(2):
                    when(t_act[s], 6, na)
                    done(s, dve.tensor_reduce(row(s, 9), score[:, PART[s], :], AX.X, ALU.add))
                for s in range(2):
                    settled(s)
                    done(s, dve.reciprocal(row(s, 10), row(s, 9)))
                for s in range(2):
                    settled(s)
                    done(s, dve.tensor_tensor(row(s, 11), row(s, 10), row(s, 13), ALU.mult))
                for s in range(2):
                    settled(s)
                    for b in range(2):
                        half = slice(b * 64, (b + 1) * 64)
                        done(s, dve.tensor_tensor(prob_bd[half, PART[s], half], score[half, PART[s], :],
                                                  row(s, 11)[half].unsqueeze(2).to_broadcast([64, HT, 64]), ALU.mult), ("p0", "p")[b])
                for s in range(2):
                    when(t_pe[s], 8, npe)
                    done(s, dve.tensor_copy(o_t[0:D, COLS[s]], bank[0:D, 4 + s, :]), "o")
                for s in range(2):
                    when(t_pe[s], 9, npe)
                    done(s, dve.tensor_tensor(tok_h2[:, PART[s], :], tok_h[:, PART[s], :], tiles(s, 6), ALU.add), "h2")
                norm(tok_n2, tok_h2, 2)
                for s in range(2):
                    settled(s)
                    done(s, dve.tensor_copy(n2_hl[:, PART[s], 0, :], tok_n2[:, PART[s], :]))
                for s in range(2):
                    settled(s)
                    done(s, dve.tensor_tensor(n2_hl[:, PART[s], 1, :], tok_n2[:, PART[s], :], n2_hl[:, PART[s], 0, :].bitcast(f32),
                                              ALU.subtract), "n2_hl")
                for s in range(2):
                    when(t_pe[s], 11, npe)
                    done(s, dve.tensor_tensor(logit[:, PART[s], :], bank[:, 2 + s, 0:HT * E].rearrange("p (t e) -> p t e", t=HT),
                                              gateb_sb[:, :].unsqueeze(1).to_broadcast([128, HT, E]), ALU.add))
                for s in range(2):
                    settled(s)
                    dve.sem_inc(tail_passed, 1)
                    for t in TILES[s]:
                        done(s, dve.max(top8[:, t, :], logit[:, t, :]))
                for s in range(2):
                    settled(s)
                    done(s, dve.tensor_tensor(row(s, 7), top8[:, PART[s], 1], top8[:, PART[s], 0], ALU.subtract), "diff")
                for s in range(2):
                    for t in TILES[s]:
                        done(s, dve.max_index(idx_u[:, t, :], top8[:, t, :], logit[:, t, :]))
                for s in range(2):
                    settled(s)
                    done(s, dve.tensor_copy(idx_f[:, PART[s], :], idx_u[:, PART[s], :]))
                iota = iota_f[:, :].unsqueeze(1).to_broadcast([128, HT, E])
                for s in range(2):
                    settled(s)
                    done(s, dve.tensor_tensor(oh1[:, PART[s], :], iota, wide(idx_f[:, PART[s], 0], E), ALU.is_equal))
                    done(s, dve.tensor_tensor(oh2[:, PART[s], :], iota, wide(idx_f[:, PART[s], 1], E), ALU.is_equal))
                for s in range(2):
                    when(t_act[s], 10, na)
                    done(s, dve.tensor_scalar(row(s, 9), row(s, 8), 1.0, None, ALU.add))
                for s in range(2):
                    settled(s)
                    done(s, dve.reciprocal(row(s, 10), row(s, 9)))
                for s in range(2):
                    settled(s)
                    done(s, dve.tensor_tensor(row(s, 11), row(s, 10), row(s, 8), ALU.mult))
                for s in range(2):
                    settled(s)
                    for k, oh in ((10, oh1), (11, oh2)):
                        done(s, dve.tensor_tensor(oh[:, PART[s], :], oh[:, PART[s], :], wide(row(s, k), E), ALU.mult))
                for s in range(2):
                    settled(s)
                    done(s, dve.tensor_tensor(gate[:, PART[s], :], oh1[:, PART[s], :], oh2[:, PART[s], :], ALU.add))
                for s in range(2):
                    settled(s)
                    done(s, dve.tensor_copy(gate_hl[:, PART[s], 0, :], gate[:, PART[s], :]))
                for s in range(2):
                    settled(s)
                    done(s, dve.tensor_tensor(gate_hl[:, PART[s], 1, :], gate[:, PART[s], :], gate_hl[:, PART[s], 0, :].bitcast(f32),
                                              ALU.subtract), "g")

                def weigh(k):
                    dve.wait_ge(relu_done, c * steps + k + 1)
                    if k >= 3:
                        dve.wait_ge(high_done, c * steps + k - 2)
                        dve.wait_ge(low_done, c * steps + k - 2)
                    dve.tensor_tensor(gated[k % 3][:, :], relu[k % 3][:, :], bank[:, GATE_BANK[k % 3], :],
                                      ALU.mult).then_inc(gated_done, 1)

                def low(k):
                    dve.wait_ge(high_done, c * steps + k + 1)
                    if k >= 3:
                        dve.wait_ge(down_done, c * steps + k - 2)
                    dve.tensor_tensor(gated_l[k % 3][:, :], gated[k % 3][:, :], gated_h[k % 3][:, :].bitcast(f32),
                                      ALU.subtract).then_inc(low_done, 1)

                weigh(0)
                for k in range(1, steps):
                    weigh(k)
                    low(k - 1)
                low(steps - 1)
                def z(s):
                    return bank[:, s, :].rearrange("p (t a d) -> p t a d", t=HT, a=2)

                for s in range(2):
                    when(t_pe[s], 13, npe)
                    done(s, dve.tensor_tensor(acc1[:, PART[s], :], tok_n2[:, PART[s], :], z(s)[:, :, 0, :], ALU.add))
                for s in range(2):
                    settled(s)
                    done(s, dve.tensor_tensor(acc2[:, PART[s], :], acc1[:, PART[s], :], z(s)[:, :, 1, :], ALU.add))
                norm(acc1, acc2, 3)
                for s in range(2):
                    settled(s)
                    done(s, dve.tensor_tensor(acc2[:, PART[s], :], acc1[:, PART[s], :],
                                              gb_sb[:, 0, :].unsqueeze(1).to_broadcast([128, HT, D]), ALU.mult))
                for s in range(2):
                    settled(s)
                    done(s, dve.tensor_tensor(acc1[:, PART[s], :], acc2[:, PART[s], :],
                                              gb_sb[:, 1, :].unsqueeze(1).to_broadcast([128, HT, D]), ALU.add))
                dve.wait_ge(st_out, c * 16 + 1)
                for s in range(2):
                    settled(s)
                    done(s, dve.tensor_tensor(tok_o[:, PART[s], :], acc1[:, PART[s], :], tok_h2[:, PART[s], :], ALU.add))
                assert count == [nd, nd], count


def kernel(**inputs):
    import numpy as _np
    import concourse.bacc as _bacc
    from concourse import mybir as _mybir
    from concourse.bass_utils import run_bass_kernel_spmd as _run

    a = {k: _np.asarray(v) for k, v in inputs.items()}
    f = _np.float32
    tok, at, ff = "L0_tok_", "L0_attn_", "L0_ffn_"
    w4 = _np.arange(4)
    xq = a["x"].reshape(IMAGES // Q, Q, H, 2, WL, 3)
    x_rows = xq.transpose(0, 3, 2, 1, 5, 4).reshape(IMAGES // Q, 128, Q * 96)
    x_cols = _np.ones((IMAGES // Q, 97, Q * 128), f)
    x_cols[:, 0:96] = xq.transpose(0, 4, 5, 1, 3, 2).reshape(IMAGES // Q, 96, Q * 128)
    mix = _np.zeros((LAYERS, KHH, MODES, 4, C, C), f)
    conv = _np.zeros((C, 4, LAYERS, C, 4), f)
    for l in range(LAYERS):
        sw = a[f"{tok}sw{l}"].reshape(C, C, KHH, 4, MODES)
        for q in range(4):
            mix[l, :, :, q] = sw[:, :, :, q, :].transpose(2, 3, 0, 1)
            conv[:, q, l, :, q] = a[f"{tok}cw{l}"].T
    mix = mix.reshape(LAYERS * MIXS, MIXN, 128, C).transpose(0, 2, 1, 3).reshape(LAYERS * MIXS, 128, MIXN * C)
    convb = _np.stack([a[f"{tok}cb{l}"] for l in range(LAYERS)], 1)
    fc0 = _np.zeros((97, 8, C, 4), f)
    for w in range(WL):
        fc0[3 * w:3 * w + 3, w // 4, :, w % 4] = a[tok + "fc0_w"]
    fc0[96] = a[tok + "fc0_b"][None, :, None]
    fc0s = _np.zeros((97, KHH, 4, C), f)
    for kh in range(MODES):
        fc0s[3 * kh:3 * kh + 3, kh // 4, kh % 4] = a[tok + "fc0_w"]
    fc0s[96, 0, 0] = a[tok + "fc0_b"]
    fc1 = _np.zeros((C, 4, 2, 2, F1F), f)
    for j in range(2):
        for q in range(2):
            fc1[:, 2 * j + q, j, q, :] = a[tok + "fc1_w"]
    fc1b = _np.concatenate([a[tok + "fc1_b"]] * 2).reshape(128, 1)
    fc2 = _np.zeros((2, F1F, 4, 4, 2), f)
    for q in range(2):
        for c in range(4):
            fc2[q, :, c, c, q] = a[tok + "fc2_w"][:, 0]

    def below(w, b):
        return _np.concatenate([w, b.reshape(1, -1)], 0)

    wq, bq, wk, bk = a[at + "Wq"], a[at + "bq"], a[at + "Wk"], a[at + "bk"]
    attn = _np.concatenate([below(wq.T, bq), below(wk.T, bk), below(a[at + "Wv"].T, a[at + "bv"]),
                            below(wq[0:1].T, bq[0:1]), below(wk[0:1].T, bk[0:1]),
                            below(a[at + "Wo"].T, a[at + "bo"])], 1)
    w1 = a[ff + "w1"].transpose(1, 0, 2).reshape(D, E * F)
    w2 = a[ff + "w2"].transpose(1, 0, 2).reshape(F, E * D)
    sel = _np.tile(_np.eye(E, dtype=f), (2, 1))[:, :, None].repeat(128, 2).reshape(2 * E, E * 128)
    arrays = {
        "x_rows": x_rows, "x_cols": x_cols, "dft": dft_constants(), "mix_w": mix,
        "conv_w": conv.reshape(128, LAYERS, 128), "conv_b": convb,
        "fc0_w": fc0.reshape(97, 1024), "fc0_spec": fc0s.reshape(97, KHH * 128),
        "fc1_w": fc1.reshape(128, 2, 128), "fc1_b": fc1b, "fc2_w": fc2.reshape(128, 4, 8),
        "fc2_b": a[tok + "fc2_b"].reshape(1, 1), "attn_w": attn,
        "moe_w1": _np.concatenate([w1, w1]), "moe_b1": a[ff + "b1"].T, "moe_w2": w2,
        "moe_b2": _np.concatenate([a[ff + "b2"]] * 2), "gate_w": _np.concatenate([a[ff + "gate_w"]] * 2),
        "gate_b": a[ff + "gate_b"].reshape(1, E), "selector": sel, "eye": _np.eye(128, dtype=f),
        "column_order": _np.eye(D, dtype=f).reshape(2, 2, 4, 4, D).transpose(1, 3, 2, 0, 4).reshape(D, D),
        "ln_gb": _np.stack([a[ff + "gamma"], a[ff + "beta"]]),
    }
    nc = _bacc.Bacc("TRN2", target_bir_lowering=False, num_devices=1)
    feed, args = {}, []
    for name, v in arrays.items():
        v = _np.ascontiguousarray(v)
        feed[f"in_{name}"] = v
        args.append(nc.dram_tensor(f"in_{name}", v.shape, _mybir.dt.from_np(v.dtype), kind="ExternalInput").ap())
    out = nc.dram_tensor("out_h", (IMAGES, H, W), _mybir.dt.float32, kind="ExternalOutput").ap()
    h_dram = nc.dram_tensor("h_tokens", (IMAGES, H, W), _mybir.dt.float32, kind="Internal").ap()
    token_tower(nc, *args[:12], h_dram)
    attention_and_experts(nc, h_dram, *args[12:], out)
    r = _run(nc, [feed], core_ids=[0])
    return r.results[0]["out_h"]
```
